# Optimizing a Trainium2 kernel written in Bass

```python
import numpy as np
import jax
import jax.numpy as jnp

def _softmax(x, axis=-1):
    return jax.nn.softmax(x, axis=axis)

def _gelu(x):
    return jax.nn.gelu(x, approximate=True)

def _silu(x):
    return jax.nn.silu(x)

def _sigmoid(x):
    return jax.nn.sigmoid(x)

def _layernorm(x, axis=-1, eps=1e-05):
    m = jnp.mean(x, axis=axis, keepdims=True)
    v = jnp.var(x, axis=axis, keepdims=True)
    return (x - m) / jnp.sqrt(v + eps)

def _scatter_add(tgt, idx, src, axis=0):
    return tgt.at[idx].add(src)

def _segment_sum(src, seg, n):
    return jax.ops.segment_sum(src, seg, n)
kernel_name = 'mk_prb_d1_jaxref_r8_3b51a7'

def setup_inputs(seed: int=0):
    np.random.seed(seed)
    _w = jnp.asarray

    def _L0_attn_setup():
        import jax, jax.numpy as jnp
        import numpy as np
        B, S, D, H = (2, 256, 256, 16)
        HD = D // H
        key = jax.random.key(seed)
        ks = jax.random.split(key, 5)
        scale = 0.02
        return {'hidden_states': jax.random.normal(ks[0], (B, S, D), dtype=jnp.float32), 'Wqkv_w': jax.random.normal(ks[1], (3 * D, D), dtype=jnp.float32) * scale, 'Wqkv_b': jax.random.normal(ks[2], (3 * D,), dtype=jnp.float32) * scale, 'out_w': jax.random.normal(ks[3], (D, D), dtype=jnp.float32) * scale, 'out_b': jax.random.normal(ks[4], (D,), dtype=jnp.float32) * scale}
    _L0_attn_in = _L0_attn_setup()

    def _L0_ffn_setup():
        import jax, jax.numpy as jnp
        import numpy as np
        CAP_FACTOR = 1.25
        MIN_CAPACITY = 4

        def _capacity(num_tokens, num_experts):
            cap = int(np.floor(CAP_FACTOR * num_tokens / num_experts))
            cap += cap % 2
            return max(cap, MIN_CAPACITY)
        key = jax.random.key(seed)
        k1, k2, k3, k4 = jax.random.split(key, 4)
        B, S, H, I, E = (4, 256, 256, 1024, 8)
        inputs = jax.random.normal(k1, (B, S, H), dtype=jnp.float32)
        gate_weight = jax.random.normal(k2, (E, H), dtype=jnp.float32) * np.sqrt(0.1 / H)
        wi = jax.random.normal(k3, (E, H, I), dtype=jnp.float32) * np.sqrt(0.1 / H)
        wo = jax.random.normal(k4, (E, I, H), dtype=jnp.float32) * np.sqrt(0.1 / I)
        return {'inputs': inputs, 'gate_weight': gate_weight, 'wi': wi, 'wo': wo}
    _L0_ffn_in = _L0_ffn_setup()
    _d = {'L0_attn_hidden_states': _L0_attn_in['hidden_states'], 'L0_attn_Wqkv_w': _L0_attn_in['Wqkv_w'], 'L0_attn_Wqkv_b': _L0_attn_in['Wqkv_b'], 'L0_attn_out_w': _L0_attn_in['out_w'], 'L0_attn_out_b': _L0_attn_in['out_b'], 'L0_ffn_gate_weight': _L0_ffn_in['gate_weight'], 'L0_ffn_wi': _L0_ffn_in['wi'], 'L0_ffn_wo': _L0_ffn_in['wo']}
    _x0 = _d['L0_attn_hidden_states']
    _d['L0_attn_hidden_states'] = jax.random.normal(jax.random.fold_in(jax.random.key(seed), 1), (4, 512, 256), dtype=_x0.dtype)
    del _x0
    return _d

def reference(L0_attn_hidden_states, L0_attn_Wqkv_w, L0_attn_Wqkv_b, L0_attn_out_w, L0_attn_out_b, L0_ffn_gate_weight, L0_ffn_wi, L0_ffn_wo):

    def _L0_attn_ref(hidden_states, Wqkv_w, Wqkv_b, out_w, out_b):
        import jax, jax.numpy as jnp
        import numpy as np
        B, S, D, H = (2, 256, 256, 16)
        HD = D // H
        b, s, d = hidden_states.shape
        qkv = hidden_states @ Wqkv_w.T + Wqkv_b
        qkv = qkv.reshape(b, s, 3, H, HD)
        q, k, v = (qkv[:, :, 0], qkv[:, :, 1], qkv[:, :, 2])
        softmax_scale = 1.0 / np.float32(np.sqrt(HD))
        scores = jnp.einsum('bthd,bshd->bhts', q, k) * softmax_scale
        attn = jax.nn.softmax(scores, axis=-1)
        ctx = jnp.einsum('bhts,bshd->bthd', attn, v)
        ctx = ctx.reshape(b, s, d)
        return ctx @ out_w.T + out_b

    def _L0_ffn_ref(inputs, gate_weight, wi, wo):
        import jax, jax.numpy as jnp
        import numpy as np
        CAP_FACTOR = 1.25
        MIN_CAPACITY = 4

        def _capacity(num_tokens, num_experts):
            cap = int(np.floor(CAP_FACTOR * num_tokens / num_experts))
            cap += cap % 2
            return max(cap, MIN_CAPACITY)
        E, H = gate_weight.shape
        tokens = inputs.reshape(-1, H)
        T = tokens.shape[0]
        C = _capacity(T, E)
        gate_logits = tokens @ gate_weight.T
        gate = gate_logits.astype(jnp.float32)
        probs = jax.nn.softmax(gate, axis=-1)
        top1_idx = jnp.argmax(gate, axis=-1)
        mask = jax.nn.one_hot(top1_idx, E, dtype=jnp.int32)
        ranks = jnp.cumsum(mask, axis=0) - mask
        mask = mask * (ranks < C).astype(jnp.int32)
        rank1 = jnp.sum(mask * ranks, axis=-1)
        rank_oh = jax.nn.one_hot(rank1, C, dtype=inputs.dtype)
        weight = mask.astype(inputs.dtype) * probs.astype(inputs.dtype)
        combine_weights = weight[:, :, None] * rank_oh[:, None, :]
        sec_mask_f = (combine_weights != 0).astype(inputs.dtype)
        dispatch_data = jnp.einsum('tec,th->ech', sec_mask_f, tokens)
        h = jnp.einsum('ech,ehi->eci', dispatch_data, wi)
        h = jax.nn.gelu(h, approximate=False)
        expert_out = jnp.einsum('eci,eih->ech', h, wo)
        ans = jnp.einsum('tec,ech->th', combine_weights, expert_out)
        return ans.reshape(inputs.shape)
    x = L0_attn_hidden_states
    xn = _layernorm(x, axis=-1)
    x = x + _L0_attn_ref(xn, L0_attn_Wqkv_w, L0_attn_Wqkv_b, L0_attn_out_w, L0_attn_out_b) + _L0_ffn_ref(xn, L0_ffn_gate_weight, L0_ffn_wi, L0_ffn_wo)
    return x

_drawn_inputs = setup_inputs


def setup_inputs(seed=0):
    import zlib

    import numpy as np

    out = dict(_drawn_inputs(seed))
    spreads = {}
    factors = {'L0_attn_Wqkv_w': 8.0,
     'L0_attn_Wqkv_b': 7.451,
     'L0_attn_out_w': 5.837,
     'L0_attn_out_b': 12.34,
     'L0_ffn_gate_weight': 5.624,
     'L0_ffn_wi': 5.288,
     'L0_ffn_wo': 5.146}
    for name, (base, spread) in spreads.items():
        noise = np.random.default_rng([zlib.crc32(name.encode()), seed]).standard_normal(out[name].shape)
        drawn = base * np.exp(spread * noise) if base else spread * noise
        out[name] = jnp.asarray(drawn.astype(out[name].dtype))
    for name, factor in factors.items():
        out[name] = (out[name] * factor).astype(out[name].dtype)
    return out
```

```python
from contextlib import ExitStack

import concourse.bass as bass
from concourse import mybir

F32 = mybir.dt.float32
F32R = mybir.dt.float32r
BF16 = mybir.dt.bfloat16
I32 = mybir.dt.int32
ALU = mybir.AluOpType
ACT = mybir.ActivationFunctionType
AX_X = mybir.AxisListType.X
P = 128

Q_TERMS = (0, 0, 1, 1, 0, 2)
K_TERMS = (0, 1, 0, 1, 2, 0)


def before(index, limit):
    return index < limit if isinstance(index, int) else True


def after(index, limit):
    return index > limit if isinstance(index, int) else True


def transformer_block(nc, x_in, wqkv_in, bqkv_in, wo_in, bo_in, gate_in, wi_in, wout_in, out):
    B, S, D = x_in.shape
    T = B * S
    NT = T // P
    TB = S // P
    KT = D // P
    H = 16
    HD = D // H
    E, _, FF = wi_in.shape
    CAP = int(1.25 * T / E)
    CAP += CAP % 2
    FT = FF // P
    HALF = FT // 2
    SLOTS = E * CAP
    EPS = 1e-5
    SCALE = float(HD) ** -0.5
    NTERM = len(Q_TERMS)
    MAX_ROW = NTERM * HD
    ROWS = MAX_ROW + 2
    HG = 4
    GROUPS = B * H // HG
    PAIRS = GROUPS // 2
    GPB = H // HG
    ROW_TILES = [(r, min(P, CAP - r)) for r in range(0, CAP, P)]
    VG = D + E
    QK_TILES = 2 * KT
    STACK = H * S
    assert S == 4 * P and D == 2 * P and FT == 8 and len(ROW_TILES) == 3 and GPB == 4 and HG * HD * 2 == P

    ctx = ExitStack()
    with ctx:
        def sem(name):
            return ctx.enter_context(nc.semaphore(name))

        base = (nc.sbuf_base + 31) // 32 * 32
        ARENA = 206 * 1024
        ctx.enter_context(nc.sbuf_tensor("arena", [P, ARENA // 4], F32))
        cursor = [0]

        def place(name, shape, dtype, at=None):
            size = 2 if dtype == BF16 else 4
            for n in shape[1:]:
                size *= n
            size = (size + 31) // 32 * 32
            offset = cursor[0] if at is None else at
            tensor = nc.alloc_sbuf_tensor_at(name, shape, dtype, offset=base + offset)
            if at is None:
                cursor[0] += size
                assert cursor[0] <= ARENA, (name, cursor[0])
            return tensor, offset + size

        def new(name, shape, dtype):
            return place(name, shape, dtype)[0]

        acc = new("acc", [P, NT, D], F32)
        xn = new("xn", [P, NT, D], F32)
        vg = new("vg", [P, NT, VG], F32)
        woT_h = new("woT_h", [P, KT, D], F32R)
        woT_l = new("woT_l", [P, KT, D], F32R)

        r_stack = cursor[0]
        stack = new("stack", [P, 4 * STACK], BF16)
        xT_h, at = place("xT_h", [P, B, KT, S], F32R, r_stack)
        xT_l, at = place("xT_l", [P, B, KT, S], F32R, at)
        r_second = r_stack + 4 * STACK
        wi_h, at = place("wi_h", [P, KT, FF], F32R, r_second)
        wi_l, at = place("wi_l", [P, KT, FF], F32R, at)
        wo_h, at = place("wo_h", [P, FT, D], F32R, at)
        wo_l, at = place("wo_l", [P, FT, D], F32R, at)
        assert at == r_second + 4 * STACK

        r_probs = cursor[0]
        gh, at = place("gh", [P, FT, CAP], F32R, r_probs)
        gl, at = place("gl", [P, FT, CAP], F32R, at)
        qkf, at = place("qkf", [P, 2, S], F32, at)
        qkr, at = place("qkr", [P, 2, S], F32, at)
        parts, at = place("parts", [P, 2, 3, S], BF16, at)
        cursor[0] = at
        probs, end = place("probs", [P, TB, HG, S], F32, r_probs)
        assert end <= cursor[0]

        r_weights = cursor[0]
        wT_h = new("wT_h", [P, KT, 2 * D + VG], F32R)
        wT_l = new("wT_l", [P, KT, 2 * D + VG], F32R)
        w_rows = new("w_rows", [P, 3 * KT, D], F32)
        poT, at = place("poT", [P, 2, S], F32, r_weights)
        ctx_sb, at = place("ctx_sb", [P, TB, P], F32, at)
        ctxT_h, at = place("ctxT_h", [P, S], F32R, at)
        ctxT_l, at = place("ctxT_l", [P, S], F32R, at)
        vslot, at = place("vslot", [P, 2, TB, HG, 32], F32, at)
        mrow, at = place("mrow", [32, 2, P], BF16, at)
        negm, at = place("negm", [P, 2, HG * TB], F32, at)
        mpart, at = place("mpart", [P, 2, 2, HG * TB], BF16, at)
        rsum, at = place("rsum", [P, 2, TB, HG], F32, at)
        assert at <= cursor[0]

        raw_wi = new("raw_wi", [P, KT, FF], F32)
        raw_wo = new("raw_wo", [P, FT, D], F32)
        zeros = place("zeros", [P, D], F32, cursor[0])[0]
        xd = new("xd", [P, 3, D], F32)
        gate_rows = place("gate_rows", [E, D], F32, cursor[0])[0]
        xdT_h = new("xdT_h", [P, KT, CAP], F32R)
        xdT_l = new("xdT_l", [P, KT, CAP], F32R)
        wo_rows = place("wo_rows", [P, KT, D], F32, cursor[0])[0]
        g32 = new("g32", [P, 2, CAP], F32)
        r_yT = cursor[0]
        yT = new("yT", [P, KT, CAP], F32)
        t_a, at = place("t_a", [P, NT, E], F32, r_yT)
        t_b, at = place("t_b", [P, NT, E], F32, at)
        t_c, at = place("t_c", [P, NT, E], F32, at)
        oneh, at = place("oneh", [P, NT, E], F32, at)
        assert at <= cursor[0]
        r_rows = cursor[0]
        y_rows = new("y_rows", [P, 3, D], F32)
        bvb, at = place("bvb", [P, KT, P], F32, r_rows)
        bvb_h, at = place("bvb_h", [P, KT, P], F32R, at)
        bvb_l, at = place("bvb_l", [P, KT, P], F32R, at)
        assert at <= cursor[0]

        ident = new("ident", [P, P], F32)
        identb = new("identb", [P, P], BF16)
        earlier = new("earlier", [P, P], BF16)
        onesb = new("onesb", [P, P], BF16)
        b_rows = new("b_rows", [3 * KT, P], F32)
        b_cols = new("b_cols", [P, 3 * KT], F32)
        bias = new("bias", [P, D], F32)
        stats = new("stats", [P, TB, 6], F32)
        mv = new("mv", [P, B, TB, 2], F32)
        vare = new("vare", [P, B, TB], F32)
        rstd = new("rstd", [P, B, TB], F32)
        descend = new("descend", [P, E], F32)
        starts = new("starts", [P, E], F32)
        onehb = new("onehb", [P, NT, E], BF16)
        c_a = new("c_a", [P, NT], F32)
        c_b = new("c_b", [P, NT], F32)
        c_c = new("c_c", [P, NT], F32)
        c_d = new("c_d", [P, NT], F32)
        keep = new("keep", [P, NT], F32)
        weight = new("weight", [P, NT], F32)
        dump_i = new("dump_i", [P, NT], I32)
        dump = new("dump", [P, NT], F32)
        to_slot = new("to_slot", [P, NT], I32)
        from_slot = new("from_slot", [P, NT], I32)
        y_tok = xn

        ps = ctx.enter_context(nc.psum_tensor("ps", [P, 8, 512], F32))

        parts_d = nc.dram_tensor("parts_scratch", [B, 2, 3, D, S], BF16).ap()
        xd_d = nc.dram_tensor("slots_scratch", [SLOTS + T, D], F32).ap()
        yd_d = nc.dram_tensor("expert_rows_scratch", [SLOTS, D], F32).ap()

        d_x = [sem(f"d_x{b}") for b in range(B)]
        d_w, d_small, d_zero = sem("d_w"), sem("d_small"), sem("d_zero")
        s_const, s_pool = sem("s_const"), sem("s_pool")
        s_ln, s_var, s_root, s_xn = sem("s_ln"), sem("s_var"), sem("s_root"), sem("s_xn")
        s_wT, s_wTh, s_wTl = sem("s_wT"), sem("s_wTh"), sem("s_wTl")
        s_xT, s_xTh, s_xTl = sem("s_xT"), sem("s_xTh"), sem("s_xTl")
        s_v, s_vg = sem("s_v"), sem("s_vg")
        s_route, s_exp8, s_oneh, s_rank = sem("s_route"), sem("s_exp8"), sem("s_oneh"), sem("s_rank")
        s_index = sem("s_index")
        d_scatter = sem("d_scatter")
        s_bvb, s_bvp, s_bias, s_xb = sem("s_bvb"), sem("s_bvp"), sem("s_bias"), sem("s_xb")
        s_qk, s_qkf, s_hi, s_r, s_mid, s_lo = (sem(n) for n in ("s_qk", "s_qkf", "s_hi", "s_r", "s_mid", "s_lo"))
        d_parts = [sem("d_parts0"), sem("d_parts1")]
        d_raw = [sem(f"d_raw{k}") for k in range(4)]
        w_hi = [sem(f"w_hi{k}") for k in range(4)]
        w_lo = [sem(f"w_lo{k}") for k in range(4)]
        s_yhalf = sem("s_yhalf")
        d_xd, s_xdT, s_xdh, s_xdl = sem("d_xd"), sem("s_xdT"), sem("s_xdh"), sem("s_xdl")
        s_h, s_gelu, s_gh, s_gl = sem("s_h"), sem("s_gelu"), sem("s_gh"), sem("s_gl")
        s_y, s_yT, s_yb, s_yr, d_y = sem("s_y"), sem("s_yT"), sem("s_yb"), sem("s_yr"), sem("d_y")
        d_gather, s_wy, s_comb = sem("d_gather"), sem("s_wy"), sem("s_comb")
        s_ones, d_stack = sem("s_ones"), sem("d_stack")
        s_vz, s_vslot = sem("s_vz"), sem("s_vslot")
        s_smax, s_red, s_mhi, s_msplit = sem("s_smax"), sem("s_red"), sem("s_mhi"), sem("s_msplit")
        s_mT, s_mev = sem("s_mT"), sem("s_mev")
        d_mrow = [sem("d_mrow0"), sem("d_mrow1")]
        s_st, s_exp, s_pv, s_po = sem("s_st"), sem("s_exp"), sem("s_pv"), sem("s_po")
        s_pt, s_rs, s_ctx = sem("s_pt"), sem("s_rs"), sem("s_ctx")
        s_cT, s_cTh, s_cTl = sem("s_cT"), sem("s_cTh"), sem("s_cTl")
        s_op, s_acc, d_out = sem("s_op"), sem("s_acc"), sem("d_out")

        def piece(k, wi_t, wo_t):
            half = k % 2
            if k < 2:
                return wi_t[:, :, half * HALF * P:(half + 1) * HALF * P]
            return wo_t[:, half * HALF:(half + 1) * HALF, :]

        x_tiles = x_in.rearrange("b (t p) d -> b p t d", p=P)
        out_tiles = out.rearrange("b (t p) d -> b p t d", p=P)
        wi_flat = wi_in.rearrange("e (k p) f -> p (e k) f", p=P)
        wout_flat = wout_in.rearrange("e (t p) d -> p (e t) d", p=P)
        N_QK = B * QK_TILES

        def stack_at(pair, is_k):
            p4 = pair % 4
            return p4 * 2 * HG * S + (p4 // 2) * STACK + (STACK if is_k else 0)

        def wait_used(eng, k, e):
            if k < 2:
                eng.wait_ge(s_h, FT * e + HALF * (k + 1))
            else:
                eng.wait_ge(s_yhalf if k == 2 else s_y, e + 1)

        LOADS_W, LOADS_SMALL = 4, 1
        STACK_LOADS = 2 * NTERM
        block = ctx.enter_context(nc.Block())

        @block.sync
        def _(sp):
            for b in range(B):
                sp.dma_start(acc[:, b * TB:(b + 1) * TB, :], x_tiles[b]).then_inc(d_x[b], 16)

            def load_piece(k, e):
                if after(e, 0):
                    sp.wait_ge(w_lo[k], e)
                if k < 2:
                    src = wi_flat[:, bass.ds(e * KT, KT), (k % 2) * HALF * P:(k % 2 + 1) * HALF * P]
                else:
                    src = wout_flat[:, bass.ds(e * FT + (k % 2) * HALF, HALF), :]
                sp.dma_start(piece(k, raw_wi, raw_wo), src).then_inc(d_raw[k], 16)

            def load_rows(e):
                if after(e, 0):
                    sp.wait_ge(s_xdT, e)
                sp.dma_start(xd[:, 0:2, :], xd_d[bass.ds(e * CAP, 2 * P), :].rearrange("(t p) d -> p t d", p=P)
                             ).then_inc(d_xd, 16)
                sp.dma_start(xd[0:CAP - 2 * P, 2, :], xd_d[bass.ds(e * CAP + 2 * P, CAP - 2 * P), :]).then_inc(d_xd, 16)

            def store_rows(e):
                sp.wait_ge(s_yr, 2 * e + 2)
                sp.dma_start(yd_d[bass.ds(e * CAP, 2 * P), :].rearrange("(t p) d -> p t d", p=P), y_rows[:, 0:2, :]
                             ).then_inc(d_y, 16)
                sp.dma_start(yd_d[bass.ds(e * CAP + 2 * P, CAP - 2 * P), :], y_rows[0:CAP - 2 * P, 2, :]).then_inc(d_y, 16)

            for k in (0, 1, 2, 3):
                load_piece(k, 0)
            for n in range(N_QK):
                b, m = divmod(n, QK_TILES)
                sp.wait_ge(s_lo, n + 1)
                dst = parts_d[b, m // KT].rearrange("c (m p) s -> p c m s", p=P)[:, :, m % KT, :]
                sp.dma_start(dst, parts[:, n % 2, :, :]).then_inc(d_parts[n % 2], 16)
            sp.wait_ge(d_scatter, 16 * NT)
            load_rows(0)
            load_piece(0, 1)
            load_piece(1, 1)
            load_rows(1)

            def expert(e):
                if before(e, E - 2):
                    load_rows(e + 2)
                if after(e, 0):
                    store_rows(e - 1)
                if before(e, E - 1):
                    load_piece(2, e + 1)
                    load_piece(3, e + 1)
                if before(e, E - 2):
                    load_piece(0, e + 2)
                    load_piece(1, e + 2)

            expert(0)
            with sp.Fori(1, E - 2) as e:
                expert(e)
            expert(E - 2)

            def load_stack(b):
                for which, terms in enumerate((Q_TERMS, K_TERMS)):
                    for r, part in enumerate(terms):
                        at = (b % 2) * 2 * STACK + which * STACK
                        dst = stack[r * HD:(r + 1) * HD, at:at + STACK].rearrange("p (h s) -> p h s", s=S)
                        src = parts_d[b, which, part].rearrange("(h d) s -> d h s", d=HD)
                        sp.dma_start(dst, src).then_inc(d_stack, 16)

            for n in range(2):
                sp.wait_ge(d_parts[n], 16 * (N_QK // 2))
            load_stack(0)
            expert(E - 1)
            store_rows(E - 1)
            wait_used(sp, 3, E - 1)
            sp.wait_ge(d_stack, 16 * STACK_LOADS)
            load_stack(1)

            def load_max(g, hg):
                sp.wait_ge(s_mev, g + 1)
                at = (g // GPB % 2) * 2 * STACK + hg * HG * S
                for r in range(2):
                    dst = stack[MAX_ROW + r:MAX_ROW + r + 1, at:at + HG * S].rearrange("r (c t) -> r c t", t=P)
                    sp.dma_start(dst, mrow[16 * r:16 * r + 16, g % 2, :]).then_inc(d_mrow[g % 2], 16)

            load_max(0, 0)
            for b in range(B):
                for hg in range(GPB):
                    g = GPB * b + hg + 1
                    if g < GROUPS:
                        load_max(g, g % GPB)
                    if hg == 3 and b + 2 < B:
                        sp.wait_ge(s_exp, 16 * GPB * (b + 1) + 2)
                        sp.wait_ge(d_stack, 16 * STACK_LOADS * (b + 2))
                        load_stack(b + 2)
                    if hg == 2 and b > 0:
                        sp.wait_ge(s_acc, GPB * b + 2)
                        sp.dma_start(out_tiles[b - 1], acc[:, (b - 1) * TB:b * TB, :]).then_inc(d_out, 16)
            sp.wait_ge(s_acc, GPB * B + 2)
            sp.dma_start(out_tiles[B - 1], acc[:, (B - 1) * TB:, :]).then_inc(d_out, 16)
            sp.wait_ge(d_out, 16 * B)

        @block.gpsimd
        def _(pool):
            pool.memset(ident[:], 0.0).then_inc(s_pool, 1)
            pool.memset(identb[:], 0.0).then_inc(s_pool, 1)
            pool.memset(earlier[:], 1.0).then_inc(s_pool, 1)
            pool.wait_ge(s_pool, 3)
            for m in (ident, identb):
                pool.affine_select(out=m[:], in_=m[:], compare_op=ALU.not_equal, fill=1.0, base=0,
                                   pattern=[[-1, P]], channel_multiplier=1).then_inc(s_const, 1)
            pool.affine_select(out=earlier[:], in_=earlier[:], compare_op=ALU.is_gt, fill=0.0, base=0,
                               pattern=[[1, P]], channel_multiplier=-1).then_inc(s_const, 1)
            pool.memset(onesb[:], 1.0).then_inc(s_const, 1)
            pool.memset(zeros[:], 0.0).then_inc(s_pool, 1)
            pool.wait_ge(s_pool, 4)
            per = SLOTS // P
            pool.dma_start(xd_d[0:SLOTS, :].rearrange("(p r) d -> p r d", r=per),
                           zeros[:, :].unsqueeze(1).to_broadcast([P, per, D])).then_inc(d_zero, 16)
            for e in range(E):
                pool.memset(descend[:, e:e + 1], float(E - e)).then_inc(s_const, 1)
                pool.memset(starts[:, e:e + 1], float(e * CAP)).then_inc(s_const, 1)
            pool.iota(dump_i[:], [[P, NT]], base=SLOTS, channel_multiplier=1).then_inc(s_const, 1)
            pool.wait_ge(s_wTh, 6)
            pool.memset(bvb[:], 1.0).then_inc(s_pool, 1)
            pool.wait_ge(s_pool, 5)
            for kt in range(KT):
                pool.tensor_scalar(bvb[:, kt, :], bvb[:, kt, :], b_cols[:, QK_TILES + kt:QK_TILES + kt + 1], None, ALU.mult).then_inc(s_bvb, 1)
            pool.wait_ge(s_bvb, KT)
            pool.tensor_copy(bvb_h[:], bvb[:]).then_inc(s_bvb, 1)
            pool.wait_ge(s_bvb, KT + 1)
            pool.tensor_tensor(bvb_l[:], bvb[:], bvb_h[:].bitcast(F32), ALU.subtract).then_inc(s_bvb, 1)

            pool.wait_ge(d_zero, 16)
            pool.wait_ge(s_index, 2)
            for t in range(NT):
                pool.indirect_dma_start(out=xd_d, out_offset=bass.IndirectOffsetOnAxis(ap=to_slot[:, t:t + 1], axis=0),
                                        in_=xn[:, t, :], in_offset=None).then_inc(d_scatter, 16)

            def split_low(k, e):
                pool.wait_ge(w_hi[k], e + 1)
                pool.tensor_tensor(piece(k, wi_l, wo_l), piece(k, raw_wi, raw_wo), piece(k, wi_h, wo_h).bitcast(F32),
                                   ALU.subtract).then_inc(w_lo[k], 1)

            for n in range(N_QK):
                pool.wait_ge(s_mid, n + 1)
                pool.tensor_tensor(parts[:, n % 2, 2, :], qkr[:, n % 2, :], parts[:, n % 2, 1, :], ALU.subtract
                                   ).then_inc(s_lo, 1)
                if n == 8:
                    split_low(2, 0)

            def expert(e):
                split_low(3, e)
                if before(e, E - 1):
                    split_low(2, e + 1)

            with pool.Fori(0, E - 1) as e:
                expert(e)
            expert(E - 1)
            pool.wait_ge(s_bias, 1)
            for b in range(B):
                t0 = b * TB
                pool.tensor_tensor(acc[:, t0:t0 + TB, :], acc[:, t0:t0 + TB, :],
                                   bias[:, :].unsqueeze(1).to_broadcast([P, TB, D]), ALU.add).then_inc(s_xb, 1)

            pool.wait_ge(s_qk, N_QK)
            pool.wait_ge(s_bias, 1)
            pool.memset(vslot[:], 0.0).then_inc(s_vz, 1)
            pool.wait_ge(s_vz, 1)
            pool.memset(vslot[:, :, :, :, HD:HD + 1], 1.0).then_inc(s_vz, 1)

            def copy_v(pair, u):
                g = 2 * pair + u
                if after(g, 1):
                    pool.wait_ge(s_pv, TB * g - TB)
                src = vg[:, bass.ds(pair // 2 * TB, TB), bass.ds(pair % 2 * 2 * HG * HD + u * HG * HD, HG * HD)]
                pool.tensor_copy(vslot[:, u, :, :, 0:HD], src.rearrange("p t (j c) -> p t j c", j=HG)
                                 ).then_inc(s_vslot, 1)

            pool.wait_ge(s_vz, 2)
            copy_v(0, 0)
            copy_v(0, 1)
            pool.wait_ge(d_y, 32 * E)
            for t in range(NT):
                pool.indirect_dma_start(out=y_tok[:, t, :], out_offset=None, in_=yd_d,
                                        in_offset=bass.IndirectOffsetOnAxis(ap=from_slot[:, t:t + 1], axis=0)
                                        ).then_inc(d_gather, 16)
            pool.wait_ge(d_gather, 16 * NT)
            pool.wait_ge(s_xb, B)
            for b in range(B):
                tiles = slice(b * TB, (b + 1) * TB)
                pool.tensor_tensor(y_tok[:, tiles, :], y_tok[:, tiles, :],
                                   weight[:, tiles].unsqueeze(2).to_broadcast([P, TB, D]), ALU.mult).then_inc(s_wy, 1)
                pool.wait_ge(s_wy, b + 1)
                pool.tensor_tensor(acc[:, tiles, :], acc[:, tiles, :], y_tok[:, tiles, :], ALU.add).then_inc(s_comb, 1)
            with pool.Fori(1, PAIRS) as p:
                copy_v(p, 0)
                copy_v(p, 1)

        @block.scalar
        def _(act):
            act.dma_start(w_rows[:], wqkv_in.rearrange("(m p) d -> p m d", p=P)).then_inc(d_w, 16)
            act.dma_start(wo_rows[:], wo_in.rearrange("(m p) d -> p m d", p=P)).then_inc(d_w, 16)
            act.dma_start(gate_rows[:], gate_in).then_inc(d_w, 16)
            act.dma_start(b_rows[:], bqkv_in.rearrange("(m p) -> m p", p=P)).then_inc(d_w, 16)
            act.dma_start(bias[:], bo_in.rearrange("(a d) -> a d", a=1).to_broadcast([P, D])).then_inc(d_small, 16)

            def weight_banks():
                for kt in range(KT):
                    yield wT_h[:, kt, 0:512], ps[:, 2 + kt, :]
                for kt in range(KT):
                    yield wT_h[:, kt, 512:512 + VG], ps[:, 4 + kt, 0:VG]
                yield woT_h[:], ps[:, 6, :].rearrange("p (k d) -> p k d", k=KT)
                yield b_cols[:], ps[:, 7, 0:3 * KT]

            def root(b):
                act.wait_ge(s_var, b + 1)
                act.activation(vare[:, b, :], vare[:, b, :], ACT.Sqrt).then_inc(s_root, 1)

            root(0)
            root(1)
            for n, (dst, src) in enumerate(weight_banks()):
                act.wait_ge(s_wT, n + 1)
                act.activation(dst, src, ACT.Copy).then_inc(s_wTh, 1)

            def split_high(k, e):
                act.wait_ge(d_raw[k], 16 * e + 16)
                if after(e, 0):
                    wait_used(act, k, e - 1)
                act.activation(piece(k, wi_h, wo_h), piece(k, raw_wi, raw_wo), ACT.Copy).then_inc(w_hi[k], 1)

            for b in range(B):
                if b + 2 < B:
                    root(b + 2)
                act.wait_ge(s_xT, b + 1)
                act.activation(xT_h[:, b, :, :], ps[:, 0:2, :], ACT.Copy).then_inc(s_xTh, 1)
                for t in range(b * TB, (b + 1) * TB):
                    act.wait_ge(s_v, t + 1)
                    act.activation(vg[:, t, :], ps[:, 2 + t % 2, 0:VG], ACT.Copy).then_inc(s_vg, 1)
            act.wait_ge(s_route, 2)
            act.activation(t_b[:], t_a[:], ACT.Exp).then_inc(s_exp8, 1)
            act.wait_ge(s_wTh, 6)

            def middle_part(n):
                act.wait_ge(s_r, n + 1)
                act.activation(parts[:, n % 2, 1, :], qkr[:, n % 2, :], ACT.Copy).then_inc(s_mid, 1)

            for n in range(N_QK):
                act.wait_ge(s_qk, n + 1)
                if n >= 2:
                    act.wait_ge(s_r, n - 1)
                act.activation(qkf[:, n % 2, :], ps[:, 4 + n % 2, :], ACT.Identity,
                               bias=b_cols[:, n % QK_TILES:n % QK_TILES + 1]).then_inc(s_qkf, 1)
                if n:
                    middle_part(n - 1)
                if n in (4, 5, 6):
                    split_high((0, 1, 2)[n - 4], 0)
            middle_part(N_QK - 1)

            def rows_high(e):
                act.wait_ge(s_xdT, e + 1)
                if after(e, 0):
                    wait_used(act, 1, e - 1)
                act.activation(xdT_h[:], ps[:, 4:6, 0:CAP], ACT.Copy).then_inc(s_xdh, 1)

            def gelu(e, i):
                n = FT * e + i
                act.wait_ge(s_h, n + 1)
                if after(n, 1):
                    act.wait_ge(s_gl, n - 1)
                act.activation(g32[:, i % 2, :], ps[:, i % 2, 0:CAP], ACT.Gelu).then_inc(s_gelu, 1)

            def expert(e):
                for i in range(FT):
                    gelu(e, i)
                    if i == 1:
                        split_high(3, e)
                    if i == 5 and before(e, E - 1):
                        split_high(0, e + 1)
                if before(e, E - 1):
                    split_high(1, e + 1)
                    rows_high(e + 1)
                    split_high(2, e + 1)
                act.wait_ge(s_y, e + 1)
                if after(e, 0):
                    act.wait_ge(s_yb, e)
                act.activation(yT[:], ps[:, 2:4, 0:CAP], ACT.Copy).then_inc(s_yT, 1)

            rows_high(0)
            expert(0)
            with act.Fori(1, E - 1) as e:
                expert(e)
            expert(E - 1)

            def turn_max(g, u):
                act.wait_ge(s_mT, g + 1)
                act.activation(mrow[:, u, :], ps[0:32, 7, 0:P // 2].bitcast(BF16), ACT.Copy).then_inc(s_mev, 1)

            def take_out(g, u):
                act.wait_ge(s_pv, TB * g + TB)
                if after(g, 1):
                    act.wait_ge(s_pt, g - 1)
                act.activation(poT[:, u, :], ps[:, 6, :], ACT.Copy).then_inc(s_po, 1)

            def context_high(q):
                act.wait_ge(s_cT, q + 1)
                act.activation(ctxT_h[:], ps[:, 7, :], ACT.Copy).then_inc(s_cTh, 1)

            def group(p, u):
                g = 2 * p + u
                for st in range(TB):
                    if after(g, 0):
                        act.wait_ge(s_pv, TB * g + st + 1 - TB)
                    for j in range(HG):
                        n = 16 * g + HG * st + j
                        act.wait_ge(s_st, n + 1)
                        act.activation(probs[:, st, j, :], ps[:, 4 + j % 2, :], ACT.Exp, scale=SCALE
                                       ).then_inc(s_exp, 1)
                    if st == 0 and after(g, 0):
                        take_out(g - 1, 1 - u)
                    if st == 1 and (u == 0 or before(p, PAIRS - 1)):
                        turn_max(g + 1, 1 - u)
                if u == 0 and after(p, 0):
                    context_high(p - 1)

            act.sem_inc(s_exp, 2)
            act.wait_ge(s_vz, 2)
            turn_max(0, 0)
            act.wait_ge(s_gl, FT * E)
            wait_used(act, 3, E - 1)
            group(0, 0)
            group(0, 1)
            with act.Fori(1, PAIRS - 1) as p:
                group(p, 0)
                group(p, 1)
            group(PAIRS - 1, 0)
            group(PAIRS - 1, 1)
            take_out(GROUPS - 1, 1)
            context_high(PAIRS - 1)

        @block.vector
        def _(dve):
            ln, route = [0], [0]

            def chain(counter, semaphore, instruction):
                instruction.then_inc(semaphore, 1)
                counter[0] += 1
                dve.wait_ge(semaphore, counter[0])

            def statistics(b):
                dve.wait_ge(d_x[b], 16)
                for t in range(TB):
                    last = dve.bn_stats(stats[:, t, :], acc[:, b * TB + t, :])
                chain(ln, s_ln, last)
                for t in range(TB):
                    last = dve.bn_aggr(mv[:, b, t, :], stats[:, t, :])
                chain(ln, s_ln, last)
                dve.tensor_scalar(vare[:, b, :], mv[:, b, :, 1], EPS, None, ALU.add).then_inc(s_var, 1)

            def normalise_tokens(b):
                dve.wait_ge(s_root, b + 1)
                chain(ln, s_ln, dve.reciprocal(rstd[:, b, :], vare[:, b, :]))
                for t in range(TB):
                    last = dve.tensor_scalar(xn[:, b * TB + t, :], acc[:, b * TB + t, :], mv[:, b, t, 0:1],
                                             rstd[:, b, t:t + 1], ALU.subtract, ALU.mult)
                last.then_inc(s_xn, 1)

            def weight_banks():
                for kt in range(KT):
                    yield wT_l[:, kt, 0:512], ps[:, 2 + kt, :], wT_h[:, kt, 0:512]
                for kt in range(KT):
                    yield wT_l[:, kt, 512:512 + VG], ps[:, 4 + kt, 0:VG], wT_h[:, kt, 512:512 + VG]
                yield woT_l[:], ps[:, 6, :].rearrange("p (k d) -> p k d", k=KT), woT_h[:]

            statistics(0)
            statistics(1)
            normalise_tokens(0)
            for n, (dst, src, high) in enumerate(weight_banks()):
                dve.wait_ge(s_wTh, n + 1)
                dve.tensor_tensor(dst, src, high.bitcast(F32), ALU.subtract).then_inc(s_wTl, 1)
            for b in range(B):
                if b + 2 < B:
                    statistics(b + 2)
                if b + 1 < B:
                    normalise_tokens(b + 1)
                dve.wait_ge(s_xTh, b + 1)
                dve.tensor_tensor(xT_l[:, b, :, :], ps[:, 0:2, :], xT_h[:, b, :, :].bitcast(F32), ALU.subtract
                                  ).then_inc(s_xTl, 1)
            dve.wait_ge(s_bvp, 1)
            dve.wait_ge(d_small, 16 * LOADS_SMALL)
            dve.tensor_tensor(bias[:], ps[:, 7, 0:D], bias[:], ALU.add).then_inc(s_bias, 1)

            def per_tile(column):
                return column[:].unsqueeze(2).to_broadcast([P, NT, E])

            def per_expert(row):
                return row[:, :].unsqueeze(1).to_broadcast([P, NT, E])

            dve.wait_ge(s_vg, NT)
            dve.wait_ge(s_const, 4 + 2 * E + 1)
            logits = vg[:, :, D:D + E]
            chain(route, s_route, dve.tensor_reduce(c_a[:], logits, AX_X, ALU.max))
            chain(route, s_route, dve.tensor_tensor(t_a[:], logits, per_tile(c_a), ALU.subtract))
            chain(route, s_route, dve.tensor_scalar(t_c[:], t_a[:], 0.0, None, ALU.is_equal))
            chain(route, s_route, dve.tensor_tensor(t_c[:], t_c[:], per_expert(descend), ALU.mult))
            chain(route, s_route, dve.tensor_reduce(c_b[:], t_c[:], AX_X, ALU.max))
            chain(route, s_route, dve.tensor_tensor(oneh[:], t_c[:], per_tile(c_b), ALU.is_equal))
            dve.tensor_copy(onehb[:], oneh[:]).then_inc(s_oneh, 1)
            dve.wait_ge(s_exp8, 1)
            chain(route, s_route, dve.tensor_reduce(c_a[:], t_b[:], AX_X, ALU.add))
            chain(route, s_route, dve.reciprocal(weight[:], c_a[:]))
            dve.wait_ge(s_rank, 1)
            within = ps[:, 6, 0:NT * E].rearrange("p (t e) -> p t e", e=E)
            counts = ps[:, 6, 256:256 + NT * E].rearrange("p (t e) -> p t e", e=E)
            chain(route, s_route, dve.memset(t_a[:, 0:1, :], 0.0))
            chain(route, s_route, dve.tensor_copy(t_a[:, 1:NT, :], counts[:, 0:NT - 1, :]))
            src, dst = t_a, t_b
            for step in (1, 2, 4, 8):
                chain(route, s_route, dve.tensor_copy(dst[:, 0:step, :], src[:, 0:step, :]))
                chain(route, s_route, dve.tensor_tensor(dst[:, step:NT, :], src[:, step:NT, :],
                                                        src[:, 0:NT - step, :], ALU.add))
                src, dst = dst, src
            chain(route, s_route, dve.tensor_tensor(dst[:], within, src[:], ALU.add))
            chain(route, s_route, dve.tensor_tensor(dst[:], dst[:], oneh[:], ALU.mult))
            chain(route, s_route, dve.tensor_reduce(c_b[:], dst[:], AX_X, ALU.add))
            chain(route, s_route, dve.tensor_tensor(t_c[:], oneh[:], per_expert(starts), ALU.mult))
            chain(route, s_route, dve.tensor_reduce(c_c[:], t_c[:], AX_X, ALU.add))
            chain(route, s_route, dve.tensor_scalar(keep[:], c_b[:], float(CAP), None, ALU.is_lt))
            chain(route, s_route, dve.tensor_tensor(c_c[:], c_c[:], c_b[:], ALU.add))
            chain(route, s_route, dve.tensor_copy(dump[:], dump_i[:]))
            chain(route, s_route, dve.tensor_tensor(c_d[:], c_c[:], dump[:], ALU.subtract))
            chain(route, s_route, dve.tensor_tensor(c_d[:], c_d[:], keep[:], ALU.mult))
            chain(route, s_route, dve.tensor_tensor(c_d[:], c_d[:], dump[:], ALU.add))
            dve.tensor_copy(to_slot[:], c_d[:]).then_inc(s_index, 1)
            chain(route, s_route, dve.tensor_tensor(c_a[:], c_c[:], keep[:], ALU.mult))
            dve.tensor_copy(from_slot[:], c_a[:]).then_inc(s_index, 1)
            chain(route, s_route, dve.tensor_tensor(weight[:], weight[:], keep[:], ALU.mult))

            def split_low(k, e):
                dve.wait_ge(w_hi[k], e + 1)
                dve.tensor_tensor(piece(k, wi_l, wo_l), piece(k, raw_wi, raw_wo), piece(k, wi_h, wo_h).bitcast(F32),
                                  ALU.subtract).then_inc(w_lo[k], 1)

            for n in range(N_QK):
                dve.wait_ge(s_qkf, n + 1)
                if n >= 2:
                    dve.wait_ge(d_parts[n % 2], 16 * (n // 2))
                    dve.wait_ge(s_lo, n - 1)
                dve.tensor_copy(parts[:, n % 2, 0, :], qkf[:, n % 2, :]).then_inc(s_hi, 1)
                dve.wait_ge(s_hi, n + 1)
                dve.tensor_tensor(qkr[:, n % 2, :], qkf[:, n % 2, :], parts[:, n % 2, 0, :], ALU.subtract
                                  ).then_inc(s_r, 1)
                if n in (6, 7):
                    split_low(n - 6, 0)

            def rows_low(e):
                dve.wait_ge(s_xdh, e + 1)
                dve.tensor_tensor(xdT_l[:], ps[:, 4:6, 0:CAP], xdT_h[:].bitcast(F32), ALU.subtract
                                  ).then_inc(s_xdl, 1)

            def rows_back(e):
                dve.wait_ge(s_yb, e + 1)
                if after(e, 0):
                    dve.wait_ge(d_y, 32 * e)
                dve.tensor_copy(y_rows[:, 0:2, :], ps[:, 6, :].rearrange("p (t d) -> p t d", d=D)).then_inc(s_yr, 1)
                dve.tensor_copy(y_rows[0:CAP - 2 * P, 2, :], ps[0:CAP - 2 * P, 7, 0:D]).then_inc(s_yr, 1)

            def expert(e):
                for i in range(FT):
                    n = FT * e + i
                    dve.wait_ge(s_gelu, n + 1)
                    if i % HALF == 0 and after(e, 0):
                        wait_used(dve, 2 + i // HALF, e - 1)
                    dve.tensor_copy(gh[:, i, :], g32[:, i % 2, :]).then_inc(s_gh, 1)
                    dve.wait_ge(s_gh, n + 1)
                    dve.tensor_tensor(gl[:, i, :], g32[:, i % 2, :], gh[:, i, :].bitcast(F32), ALU.subtract
                                      ).then_inc(s_gl, 1)
                    if i == 3 and after(e, 0):
                        rows_back(e - 1)
                    if i == 6 and before(e, E - 1):
                        split_low(0, e + 1)
                if before(e, E - 1):
                    split_low(1, e + 1)
                    rows_low(e + 1)

            rows_low(0)
            expert(0)
            with dve.Fori(1, E - 1) as e:
                expert(e)
            expert(E - 1)
            rows_back(E - 1)
            wait_used(dve, 3, E - 1)
            for buf in range(2):
                at = buf * 2 * STACK + STACK
                dve.memset(stack[MAX_ROW:ROWS, at:at + STACK], 1.0).then_inc(s_ones, 1)

            dve.sem_inc(s_acc, 2)

            def reduce_max(g, u, c):
                dve.wait_ge(s_smax, 8 * g + c + 1)
                col = c // 2 * TB + c % 2 * 2
                dve.tensor_reduce(negm[:, u, col:col + 2], ps[:, 2 * (c % 2):2 * (c % 2) + 2, :], AX_X, ALU.max,
                                  negate=True).then_inc(s_red, 1)

            def split_max(g, u):
                dve.wait_ge(s_red, 8 * g + 8)
                if after(g, 1):
                    dve.wait_ge(s_mT, g - 1)
                dve.tensor_copy(mpart[:, u, 0, :], negm[:, u, :]).then_inc(s_mhi, 1)
                dve.wait_ge(s_mhi, g + 1)
                dve.tensor_tensor(mpart[:, u, 1, :], negm[:, u, :], mpart[:, u, 0, :], ALU.subtract
                                  ).then_inc(s_msplit, 1)

            def normalise(g, u):
                dve.wait_ge(s_pt, g + 1)
                rows = ps[:, 7, :].rearrange("p (i j c) -> p i j c", i=TB, j=HG)
                dve.reciprocal(rsum[:, u], rows[:, :, :, HD]).then_inc(s_rs, 1)
                dve.wait_ge(s_rs, g + 1)
                dst = ctx_sb[:, :, u * HG * HD:(u + 1) * HG * HD].rearrange("p i (j c) -> p i j c", j=HG)
                dve.tensor_tensor(dst, rows[:, :, :, 0:HD], rsum[:, u].unsqueeze(3).to_broadcast([P, TB, HG, HD]),
                                  ALU.mult).then_inc(s_ctx, 1)

            def context_low(q):
                dve.wait_ge(s_cTh, q + 1)
                dve.tensor_tensor(ctxT_l[:], ps[:, 7, :], ctxT_h[:].bitcast(F32), ALU.subtract).then_inc(s_cTl, 1)

            def accumulate(q, half):
                dve.wait_ge(s_op, 2 * q + half + 1)
                tiles = acc[:, bass.ds(q // 2 * TB + 2 * half, 2), :]
                dve.tensor_tensor(tiles, ps[:, 7, :].rearrange("p (i d) -> p i d", i=2), tiles, ALU.add
                                  ).then_inc(s_acc, 1)

            def group(p, u):
                g = 2 * p + u
                more = before(p, PAIRS - 1)
                for st in range(TB):
                    if more:
                        reduce_max(g + 2, u, 2 * st)
                        reduce_max(g + 2, u, 2 * st + 1)
                    if st == 0 and u == 1 and after(p, 0):
                        accumulate(p - 1, 0)
                    if st == 2 and after(g, 0):
                        normalise(g - 1, 1 - u)
                if more:
                    split_max(g + 2, u)
                if u == 0 and after(p, 0):
                    context_low(p - 1)
                if u == 1 and after(p, 0):
                    accumulate(p - 1, 1)

            for g in range(2):
                for c in range(8):
                    reduce_max(g, g, c)
                split_max(g, g)
            group(0, 0)
            group(0, 1)
            dve.wait_ge(s_comb, B)
            with dve.Fori(1, PAIRS - 1) as p:
                group(p, 0)
                group(p, 1)
            group(PAIRS - 1, 0)
            group(PAIRS - 1, 1)
            normalise(GROUPS - 1, 1)
            context_low(PAIRS - 1)
            accumulate(PAIRS - 1, 0)
            accumulate(PAIRS - 1, 1)

        @block.tensor
        def _(pe):
            pe.wait_ge(s_const, 4)
            pe.wait_ge(d_w, 16 * LOADS_W)

            def turn(dst, src, identity):
                return pe.transpose(dst, src, identity)

            def product(dst, w_parts, x_parts, first, last):
                (wh, wl), (xh, xl) = w_parts, x_parts
                pe.matmul(dst, wh, xh, start=first, stop=False)
                pe.matmul(dst, wl, xh, start=False, stop=False)
                return pe.matmul(dst, wh, xl, start=False, stop=last)

            for kt in range(KT):
                k = slice(kt * P, (kt + 1) * P)
                for m in range(4):
                    last = turn(ps[:, 2 + kt, m * P:(m + 1) * P], w_rows[:, m, k], ident[:])
                last.then_inc(s_wT, 1)
            for kt in range(KT):
                k = slice(kt * P, (kt + 1) * P)
                for m in range(2):
                    turn(ps[:, 4 + kt, m * P:(m + 1) * P], w_rows[:, 4 + m, k], ident[:])
                turn(ps[:, 4 + kt, 2 * P:2 * P + E], gate_rows[:, k], ident[0:E, 0:E]).then_inc(s_wT, 1)
            for kt in range(KT):
                for m in range(KT):
                    last = turn(ps[:, 6, kt * D + m * P:kt * D + (m + 1) * P], wo_rows[:, m, kt * P:(kt + 1) * P], ident[:])
            last.then_inc(s_wT, 1)
            turn(ps[:, 7, 0:3 * KT], b_rows[:], ident[0:3 * KT, 0:3 * KT]).then_inc(s_wT, 1)

            def turn_tokens(b):
                pe.wait_ge(s_xn, b + 1)
                if b:
                    pe.wait_ge(s_xTl, b)
                for kt in range(KT):
                    for t in range(TB):
                        last = turn(ps[:, kt, t * P:(t + 1) * P], xn[:, b * TB + t, kt * P:(kt + 1) * P], ident[:])
                last.then_inc(s_xT, 1)

            turn_tokens(0)
            pe.wait_ge(s_wTl, 5)
            for b in range(B):
                pe.wait_ge(s_xTl, b + 1)
                if b + 1 < B:
                    turn_tokens(b + 1)
                for i in range(TB):
                    t = b * TB + i
                    if t >= 2:
                        pe.wait_ge(s_vg, t - 1)
                    for kt in range(KT):
                        col = slice(i * P, (i + 1) * P)
                        last = product(ps[:, 2 + t % 2, 0:VG], (xT_h[:, b, kt, col], xT_l[:, b, kt, col]),
                                       (wT_h[:, kt, 2 * D:], wT_l[:, kt, 2 * D:]), kt == 0, kt == KT - 1)
                    last.then_inc(s_v, 1)
            pe.wait_ge(s_bvb, KT + 2)
            for kt in range(KT):
                last = product(ps[:, 7, 0:D], (bvb_h[:, kt, :], bvb_l[:, kt, :]),
                               (woT_h[:, kt, :], woT_l[:, kt, :]), kt == 0, kt == KT - 1)
            last.then_inc(s_bvp, 1)

            def rank():
                pe.wait_ge(s_oneh, 1)
                rows = onehb[:].rearrange("p t e -> p (t e)")
                pe.matmul(ps[:, 6, 0:NT * E], earlier[:], rows, start=True, stop=True)
                pe.matmul(ps[:, 6, 256:256 + NT * E], onesb[:], rows, start=True, stop=True).then_inc(s_rank, 1)

            for n in range(N_QK):
                b, m = divmod(n, QK_TILES)
                if n == 2:
                    rank()
                if n >= 2:
                    pe.wait_ge(s_qkf, n - 1)
                for kt in range(KT):
                    col = slice(m * P, (m + 1) * P)
                    last = product(ps[:, 4 + n % 2, :], (wT_h[:, kt, col], wT_l[:, kt, col]),
                                   (xT_h[:, b, kt, :], xT_l[:, b, kt, :]), kt == 0, kt == KT - 1)
                last.then_inc(s_qk, 1)

            def turn_rows(e):
                pe.wait_ge(d_xd, 32 * e + 32)
                if after(e, 0):
                    pe.wait_ge(s_xdl, e)
                for kt in range(KT):
                    for r, (at, rows) in enumerate(ROW_TILES):
                        last = turn(ps[:, 4 + kt, at:at + rows], xd[0:rows, r, kt * P:(kt + 1) * P], ident[0:rows, 0:rows])
                last.then_inc(s_xdT, 1)

            def turn_back(e):
                pe.wait_ge(s_yT, e + 1)
                if after(e, 0):
                    pe.wait_ge(s_yr, 2 * e)
                for r, (at, rows) in enumerate(ROW_TILES):
                    for kt in range(KT):
                        to = r % 2 * D + kt * P
                        last = turn(ps[0:rows, 6 + r // 2, to:to + P], yT[:, kt, at:at + rows], ident[:])
                last.then_inc(s_yb, 1)

            def expert(e):
                for i in range(FT):
                    n = FT * e + i
                    if i % HALF == 0:
                        pe.wait_ge(w_lo[i // HALF], e + 1)
                    if i == 0:
                        pe.wait_ge(s_xdl, e + 1)
                    if after(n, 1):
                        pe.wait_ge(s_gelu, n - 1)
                    for kt in range(KT):
                        col = slice(i * P, (i + 1) * P)
                        last = product(ps[:, i % 2, 0:CAP], (wi_h[:, kt, col], wi_l[:, kt, col]),
                                       (xdT_h[:, kt, :], xdT_l[:, kt, :]), kt == 0, kt == KT - 1)
                    last.then_inc(s_h, 1)
                    if i == 2 and after(e, 0):
                        turn_back(e - 1)
                    if i == 5 and before(e, E - 1):
                        turn_rows(e + 1)
                if after(e, 0):
                    pe.wait_ge(s_yT, e)
                for i in range(FT):
                    if i % HALF == 0:
                        pe.wait_ge(w_lo[2 + i // HALF], e + 1)
                    pe.wait_ge(s_gl, FT * e + i + 1)
                    for m in range(KT):
                        col = slice(m * P, (m + 1) * P)
                        last = product(ps[:, 2 + m, 0:CAP], (wo_h[:, i, col], wo_l[:, i, col]),
                                       (gh[:, i, :], gl[:, i, :]), i == 0, i == FT - 1)
                    if i == HALF - 1:
                        last.then_inc(s_yhalf, 1)
                last.then_inc(s_y, 1)

            pe.wait_ge(s_qkf, N_QK)
            pe.wait_ge(s_vg, NT)
            turn_rows(0)
            expert(0)
            with pe.Fori(1, E - 1) as e:
                expert(e)
            expert(E - 1)
            turn_back(E - 1)

            pe.wait_ge(s_gelu, FT * E)
            pe.wait_ge(s_yT, E)
            pe.wait_ge(s_xdl, E)
            pe.wait_ge(s_yr, 2 * E)
            woT_hf, woT_lf = (m[:].rearrange("p k d -> p (k d)") for m in (woT_h, woT_l))

            def max_scores(p, u, c):
                n = 8 * (2 * p + u) + c
                if after(n, 1):
                    pe.wait_ge(s_red, n - 1)
                at = (u * HG + c // 2) * S
                for i in range(2):
                    col = at + (c % 2 * 2 + i) * P
                    last = pe.matmul(ps[:, 2 * (c % 2) + i, :], stack[0:MAX_ROW, bass.ds(stack_at(p, False) + col, P)],
                                     stack[0:MAX_ROW, bass.ds(stack_at(p, True) + at, S)], start=True, stop=True)
                last.then_inc(s_smax, 1)

            def turn_max(g, u):
                pe.wait_ge(s_msplit, g + 1)
                turn(ps[0:2 * HG * TB, 7, 0:P // 2].bitcast(BF16), mpart[:, u].rearrange("p r c -> p (r c)"), identb[:]
                     ).then_inc(s_mT, 1)

            def scores(p, u, st, j):
                n = 16 * (2 * p + u) + HG * st + j
                pe.wait_ge(s_exp, n + 1)
                at = (u * HG + j) * S
                pe.matmul(ps[:, 4 + j % 2, :], stack[0:ROWS, bass.ds(stack_at(p, True) + at + st * P, P)],
                          stack[0:ROWS, bass.ds(stack_at(p, False) + at, S)], start=True, stop=True).then_inc(s_st, 1)

            def weigh(g, u, st):
                pe.wait_ge(s_exp, 16 * g + HG * st + HG + 2)
                if st == 0:
                    pe.wait_ge(s_vslot, g + 1)
                    if after(g, 0):
                        pe.wait_ge(s_po, g)
                for j in range(HG):
                    last = pe.matmul(ps[32 * j:32 * j + 32, 6, :], vslot[:, u, st, j, :], probs[:, st, j, :],
                                     start=(st == 0), stop=(st == TB - 1))
                last.then_inc(s_pv, 1)

            def turn_out(g, u):
                pe.wait_ge(s_po, g + 1)
                for i in range(TB):
                    last = turn(ps[:, 7, i * P:(i + 1) * P], poT[:, u, i * P:(i + 1) * P], ident[:])
                last.then_inc(s_pt, 1)

            def turn_context(q):
                pe.wait_ge(s_ctx, 2 * q + 2)
                for i in range(TB):
                    last = turn(ps[:, 7, i * P:(i + 1) * P], ctx_sb[:, i, :], ident[:])
                last.then_inc(s_cT, 1)

            def project(q, half):
                rows = bass.ds(q % 2 * D, D)
                for i in range(2):
                    col = slice((2 * half + i) * P, (2 * half + i + 1) * P)
                    last = product(ps[:, 7, i * D:(i + 1) * D], (ctxT_h[:, col], ctxT_l[:, col]),
                                   (woT_hf[:, rows], woT_lf[:, rows]), True, True)
                last.then_inc(s_op, 1)

            def group(p, u):
                g = 2 * p + u
                more = before(p, PAIRS - 1)
                if more and u == 0:
                    pe.wait_ge(d_stack, 16 * STACK_LOADS * ((p + 1) // 2 + 1))
                pe.wait_ge(d_mrow[u], 32 * p + 32)
                for st in range(TB):
                    for j in range(HG):
                        scores(p, u, st, j)
                        if j % 2 and more:
                            max_scores(p + 1, u, 2 * st + j // 2)
                        if j == 1:
                            if st:
                                weigh(g, u, st - 1)
                            elif after(g, 0):
                                weigh(g - 1, 1 - u, TB - 1)
                    if st == 0 and u == 1 and after(p, 0):
                        pe.wait_ge(s_cTh, p)
                        pe.wait_ge(s_cTl, p)
                        project(p - 1, 0)
                    if st == 1 and (u == 0 or more):
                        pe.wait_ge(s_mev, g + 1)
                        if after(g, 1):
                            pe.wait_ge(s_ctx, g - 1)
                        if after(p, 0):
                            pe.wait_ge(s_acc, 2 * p + u)
                        turn_max(g + 1, 1 - u)
                    if st == 2 and after(g, 0):
                        if u == 0 or more:
                            pe.wait_ge(s_mev, g + 2)
                        else:
                            pe.wait_ge(s_acc, 2 * p + 1)
                        turn_out(g - 1, 1 - u)
                    if st == 3 and u == 0 and after(p, 0):
                        turn_context(p - 1)
                    if st == 3 and u == 1 and after(p, 0):
                        pe.wait_ge(s_ctx, g)
                        project(p - 1, 1)

            pe.wait_ge(d_stack, 16 * STACK_LOADS)
            for u in range(2):
                for c in range(8):
                    max_scores(0, u, c)
                    if u == 1 and c == 3:
                        turn_max(0, 0)
            pe.wait_ge(s_ones, 2)
            group(0, 0)
            group(0, 1)
            with pe.Fori(1, PAIRS - 1) as p:
                group(p, 0)
                group(p, 1)
            group(PAIRS - 1, 0)
            group(PAIRS - 1, 1)
            weigh(GROUPS - 1, 1, TB - 1)
            pe.wait_ge(s_acc, 2 * PAIRS)
            turn_out(GROUPS - 1, 1)
            turn_context(PAIRS - 1)
            pe.wait_ge(s_cTh, PAIRS)
            pe.wait_ge(s_cTl, PAIRS)
            project(PAIRS - 1, 0)
            pe.wait_ge(s_acc, 2 * PAIRS + 1)
            project(PAIRS - 1, 1)


_INS = ["L0_attn_hidden_states", "L0_attn_Wqkv_w", "L0_attn_Wqkv_b", "L0_attn_out_w", "L0_attn_out_b",
        "L0_ffn_gate_weight", "L0_ffn_wi", "L0_ffn_wo"]


def kernel(**inputs):
    import numpy as _np
    import concourse.bacc as _bacc
    from concourse import mybir as _mybir
    from concourse.bass_utils import run_bass_kernel_spmd as _run

    nc = _bacc.Bacc("TRN2", target_bir_lowering=False, num_devices=1)
    arrays, args = {}, []
    for name in _INS:
        a = _np.ascontiguousarray(inputs[name])
        arrays[f"in_{name}"] = a
        args.append(nc.dram_tensor(f"in_{name}", a.shape, _mybir.dt.from_np(a.dtype), kind="ExternalInput").ap())
    shape = arrays["in_" + _INS[0]].shape
    args.append(nc.dram_tensor("out_0", shape, _mybir.dt.float32, kind="ExternalOutput").ap())
    transformer_block(nc, *args)
    r = _run(nc, [arrays], core_ids=[0])
    return r.results[0]["out_0"]
```

```python
from contextlib import ExitStack

import concourse.bass as bass
from concourse import mybir

F32 = mybir.dt.float32
F32R = mybir.dt.float32r
BF16 = mybir.dt.bfloat16
I32 = mybir.dt.int32
ALU = mybir.AluOpType
ACT = mybir.ActivationFunctionType
AX_X = mybir.AxisListType.X
P = 128

Q_TERMS = (0, 0, 1, 1, 0, 2)
K_TERMS = (0, 1, 0, 1, 2, 0)


def before(index, limit):
    return index < limit if isinstance(index, int) else True


def after(index, limit):
    return index > limit if isinstance(index, int) else True


def transformer_block(nc, x_in, wqkv_in, bqkv_in, wo_in, bo_in, gate_in, wi_in, wout_in, out):
    B, S, D = x_in.shape
    T = B * S
    NT = T // P
    TB = S // P
    KT = D // P
    H = 16
    HD = D // H
    E, _, FF = wi_in.shape
    CAP = int(1.25 * T / E)
    CAP += CAP % 2
    FT = FF // P
    HALF = FT // 2
    SLOTS = E * CAP
    EPS = 1e-5
    SCALE = float(HD) ** -0.5
    NTERM = len(Q_TERMS)
    MAX_ROW = NTERM * HD
    ROWS = MAX_ROW + 2
    HG = 4
    GROUPS = B * H // HG
    PAIRS = GROUPS // 2
    GPB = H // HG
    ROW_TILES = [(r, min(P, CAP - r)) for r in range(0, CAP, P)]
    VG = D + E
    QK_TILES = 2 * KT
    RING = 8
    XT_BANKS = (0, 4)
    STACK = H * S
    assert S == 4 * P and D == 2 * P and FT == 8 and len(ROW_TILES) == 3 and GPB == 4 and HG * HD * 2 == P

    ctx = ExitStack()
    with ctx:
        def sem(name):
            return ctx.enter_context(nc.semaphore(name))

        base = (nc.sbuf_base + 31) // 32 * 32
        ARENA = 206 * 1024
        ctx.enter_context(nc.sbuf_tensor("arena", [P, ARENA // 4], F32))
        cursor = [0]

        def place(name, shape, dtype, at=None):
            size = 2 if dtype == BF16 else 4
            for n in shape[1:]:
                size *= n
            size = (size + 31) // 32 * 32
            offset = cursor[0] if at is None else at
            tensor = nc.alloc_sbuf_tensor_at(name, shape, dtype, offset=base + offset)
            if at is None:
                cursor[0] += size
                assert cursor[0] <= ARENA, (name, cursor[0])
            return tensor, offset + size

        def new(name, shape, dtype):
            return place(name, shape, dtype)[0]

        acc = new("acc", [P, NT, D], F32)
        xn = new("xn", [P, NT, D], F32)
        vg = new("vg", [P, NT, VG], F32)
        woT_h = new("woT_h", [P, KT, D], F32R)
        woT_l = new("woT_l", [P, KT, D], F32R)

        r_stack = cursor[0]
        stack = new("stack", [P, 4 * STACK], BF16)
        xT_h, at = place("xT_h", [P, B, KT, S], F32R, r_stack)
        xT_l, at = place("xT_l", [P, B, KT, S], F32R, at)
        r_second = r_stack + 4 * STACK
        wi_h, at = place("wi_h", [P, KT, FF], F32R, r_second)
        wi_l, at = place("wi_l", [P, KT, FF], F32R, at)
        wo_h, at = place("wo_h", [P, FT, D], F32R, at)
        wo_l, at = place("wo_l", [P, FT, D], F32R, at)
        assert at == r_second + 4 * STACK

        r_probs = cursor[0]
        gh, at = place("gh", [P, FT, CAP], F32R, r_probs)
        gl, end = place("gl", [P, FT, CAP], F32R, at)
        qkr, at = place("qkr", [P, 2, S], F32, r_probs)
        parts, at = place("parts", [P, RING, 3, S], BF16, at)
        probs, cursor[0] = place("probs", [P, TB, HG, S], F32, r_probs)
        assert max(at, end) <= cursor[0]

        r_weights = cursor[0]
        wT_h = new("wT_h", [P, KT, 2 * D + VG], F32R)
        wT_l = new("wT_l", [P, KT, 2 * D + VG], F32R)
        qkf = place("qkf", [P, 2, S], F32, cursor[0])[0]
        w_rows = new("w_rows", [P, 3 * KT, D], F32)
        poT, at = place("poT", [P, 2, S], F32, r_weights)
        ctx_sb, at = place("ctx_sb", [P, TB, P], F32, at)
        ctxT_h, at = place("ctxT_h", [P, S], F32R, at)
        ctxT_l, at = place("ctxT_l", [P, S], F32R, at)
        vslot, at = place("vslot", [P, 2, TB, HG, 32], F32, at)
        mrow, at = place("mrow", [32, 2, P], BF16, at)
        negm, at = place("negm", [P, 2, HG * TB], F32, at)
        mpart, at = place("mpart", [P, 2, 2, HG * TB], BF16, at)
        rsum, at = place("rsum", [P, 2, TB, HG], F32, at)
        assert at <= cursor[0]

        raw_wi = new("raw_wi", [P, KT, FF], F32)
        raw_wo = new("raw_wo", [P, FT, D], F32)
        zeros = place("zeros", [P, D], F32, cursor[0])[0]
        xd = new("xd", [P, 3, D], F32)
        gate_rows = place("gate_rows", [E, D], F32, cursor[0])[0]
        xdT_h = new("xdT_h", [P, KT, CAP], F32R)
        xdT_l = new("xdT_l", [P, KT, CAP], F32R)
        wo_rows = place("wo_rows", [P, KT, D], F32, cursor[0])[0]
        g32 = new("g32", [P, 2, CAP], F32)
        r_yT = cursor[0]
        yT = new("yT", [P, KT, CAP], F32)
        t_a, at = place("t_a", [P, NT, E], F32, r_yT)
        t_b, at = place("t_b", [P, NT, E], F32, at)
        t_c, at = place("t_c", [P, NT, E], F32, at)
        assert at <= cursor[0]
        r_rows = cursor[0]
        y_rows = new("y_rows", [P, 3, D], F32)
        bvb, at = place("bvb", [P, KT, P], F32, r_rows)
        bvb_h, at = place("bvb_h", [P, KT, P], F32R, at)
        bvb_l, at = place("bvb_l", [P, KT, P], F32R, at)
        assert at <= cursor[0]

        ident = new("ident", [P, P], F32)
        identb = new("identb", [P, P], BF16)
        earlier = new("earlier", [P, P], BF16)
        onesb = new("onesb", [P, P], BF16)
        tiles_before = new("tiles_before", [P, NT * E], BF16)
        countsb = new("countsb", [P, P], BF16)
        m_i = place("m_i", [P, NT * E], I32, r_probs)[0]
        m_low = place("m_low", [P, NT * E], I32, r_probs + 4 * NT * E)[0]
        m_same = place("m_same", [P, NT * E], F32, r_probs + 8 * NT * E)[0]
        m_later = place("m_later", [P, NT * E], F32, r_probs + 12 * NT * E)[0]
        b_rows = new("b_rows", [3 * KT, P], F32)
        b_cols = new("b_cols", [P, 3 * KT], F32)
        bias = new("bias", [P, D], F32)
        stats = new("stats", [P, TB, 6], F32)
        mv = new("mv", [P, B, TB, 2], F32)
        vare = new("vare", [P, B, TB], F32)
        rstd = new("rstd", [P, B, TB], F32)
        descend = new("descend", [P, E], F32)
        starts = new("starts", [P, E], F32)
        onehb = new("onehb", [P, NT, E], BF16)
        c_a = new("c_a", [P, NT], F32)
        c_b = new("c_b", [P, NT], F32)
        c_c = new("c_c", [P, NT], F32)
        c_d = new("c_d", [P, NT], F32)
        keep = new("keep", [P, NT], F32)
        weight = new("weight", [P, NT], F32)
        dump_i = new("dump_i", [P, NT], I32)
        warm = new("warm", [P, 1], F32)
        dump = new("dump", [P, NT], F32)
        to_slot = new("to_slot", [P, NT], I32)
        from_slot = new("from_slot", [P, NT], I32)
        y_tok = xn

        ps = ctx.enter_context(nc.psum_tensor("ps", [P, 8, 512], F32))

        parts_d = nc.dram_tensor("parts_scratch", [B, 2, 3, D, S], BF16).ap()
        xd_d = nc.dram_tensor("slots_scratch", [SLOTS + T, D], F32).ap()
        yd_d = nc.dram_tensor("expert_rows_scratch", [SLOTS, D], F32).ap()

        d_x = [sem(f"d_x{b}") for b in range(B)]
        d_w, d_small, d_zero = sem("d_w"), sem("d_small"), sem("d_zero")
        s_const, s_pool, s_warm = sem("s_const"), sem("s_pool"), sem("s_warm")
        s_ln, s_var, s_root, s_xn = sem("s_ln"), sem("s_var"), sem("s_root"), sem("s_xn")
        s_wT, s_wTh, s_wTl = sem("s_wT"), sem("s_wTh"), sem("s_wTl")
        s_xT, s_xTh, s_xTl = sem("s_xT"), sem("s_xTh"), sem("s_xTl")
        s_v, s_vg = sem("s_v"), sem("s_vg")
        s_mask, s_count, s_countb = sem("s_mask"), sem("s_count"), sem("s_countb")
        s_route, s_exp8, s_oneh, s_rank = sem("s_route"), sem("s_exp8"), sem("s_oneh"), sem("s_rank")
        s_index = sem("s_index")
        d_scatter = sem("d_scatter")
        s_bvb, s_bvp, s_bias, s_xb = sem("s_bvb"), sem("s_bvp"), sem("s_bias"), sem("s_xb")
        s_qk, s_qkf, s_r, s_mid, s_lo = sem("s_qk"), sem("s_qkf"), sem("s_r"), sem("s_mid"), sem("s_lo")
        s_hi_even, s_hi_odd = sem("s_hi_even"), sem("s_hi_odd")
        d_parts = [sem(f"d_parts{n}") for n in range(RING)]
        d_raw = [sem(f"d_raw{k}") for k in range(4)]
        w_hi = [sem(f"w_hi{k}") for k in range(4)]
        w_lo = [sem(f"w_lo{k}") for k in range(4)]
        s_yhalf = sem("s_yhalf")
        d_xd0 = sem("d_xd0")
        d_xd, s_xdT, s_xdh, s_xdl = sem("d_xd"), sem("s_xdT"), sem("s_xdh"), sem("s_xdl")
        s_h, s_gelu, s_gh, s_gl = sem("s_h"), sem("s_gelu"), sem("s_gh"), sem("s_gl")
        s_y, s_yT, s_yb, s_yr, d_y = sem("s_y"), sem("s_yT"), sem("s_yb"), sem("s_yr"), sem("d_y")
        d_gather = [sem(f"d_gather{b}") for b in range(B)]
        s_wy, s_comb = sem("s_wy"), sem("s_comb")
        d_stack = sem("d_stack")
        s_vz, s_vslot = sem("s_vz"), sem("s_vslot")
        s_smax, s_red, s_mhi, s_msplit = sem("s_smax"), sem("s_red"), sem("s_mhi"), sem("s_msplit")
        s_mT, s_mev = sem("s_mT"), sem("s_mev")
        d_mrow = [sem("d_mrow0"), sem("d_mrow1")]
        s_st, s_exp, s_pv, s_po = sem("s_st"), sem("s_exp"), sem("s_pv"), sem("s_po")
        s_pt, s_rs, s_ctx = sem("s_pt"), sem("s_rs"), sem("s_ctx")
        s_cT, s_cTh, s_cTl = sem("s_cT"), sem("s_cTh"), sem("s_cTl")
        s_op, s_acc, d_out = sem("s_op"), sem("s_acc"), sem("d_out")

        def piece(k, wi_t, wo_t):
            half = k % 2
            if k < 2:
                return wi_t[:, :, half * HALF * P:(half + 1) * HALF * P]
            return wo_t[:, half * HALF:(half + 1) * HALF, :]

        x_tiles = x_in.rearrange("b (t p) d -> b p t d", p=P)
        out_tiles = out.rearrange("b (t p) d -> b p t d", p=P)
        wi_flat = wi_in.rearrange("e (k p) f -> p (e k) f", p=P)
        wout_flat = wout_in.rearrange("e (t p) d -> p (e t) d", p=P)
        N_QK = B * QK_TILES

        def stack_at(pair, is_k):
            p4 = pair % 4
            return p4 * 2 * HG * S + (p4 // 2) * STACK + (STACK if is_k else 0)

        def wait_used(eng, k, e):
            if k < 2:
                eng.wait_ge(s_h, FT * e + HALF * (k + 1))
            else:
                eng.wait_ge(s_yhalf if k == 2 else s_y, e + 1)

        LOADS_W, LOADS_SMALL = 4, 1
        STACK_LOADS = 2 * NTERM + 1
        block = ctx.enter_context(nc.Block())

        @block.sync
        def _(sp):
            for b in range(B):
                if b == 2:
                    sp.wait_ge(d_w, 16 * LOADS_W)
                sp.dma_start(acc[:, b * TB:(b + 1) * TB, :], x_tiles[b]).then_inc(d_x[b], 16)

            def load_piece(k, e):
                if after(e, 0):
                    sp.wait_ge(w_lo[k], e)
                if k < 2:
                    src = wi_flat[:, bass.ds(e * KT, KT), (k % 2) * HALF * P:(k % 2 + 1) * HALF * P]
                else:
                    src = wout_flat[:, bass.ds(e * FT + (k % 2) * HALF, HALF), :]
                sp.dma_start(piece(k, raw_wi, raw_wo), src).then_inc(d_raw[k], 16)

            def load_rows(e):
                sp.wait_ge(s_xdT, e)
                sp.dma_start(xd[:, 0:2, :], xd_d[bass.ds(e * CAP, 2 * P), :].rearrange("(t p) d -> p t d", p=P)
                             ).then_inc(d_xd, 16)
                sp.dma_start(xd[0:CAP - 2 * P, 2, :], xd_d[bass.ds(e * CAP + 2 * P, CAP - 2 * P), :]).then_inc(d_xd, 16)

            def store_rows(e):
                sp.wait_ge(s_yr, 2 * e + 2)
                sp.dma_start(yd_d[bass.ds(e * CAP, 2 * P), :].rearrange("(t p) d -> p t d", p=P), y_rows[:, 0:2, :]
                             ).then_inc(d_y, 16)
                sp.dma_start(yd_d[bass.ds(e * CAP + 2 * P, CAP - 2 * P), :], y_rows[0:CAP - 2 * P, 2, :]).then_inc(d_y, 16)

            def load_stack(b):
                for which, terms in enumerate((Q_TERMS, K_TERMS)):
                    for r, part in enumerate(terms):
                        at = (b % 2) * 2 * STACK + which * STACK
                        dst = stack[r * HD:(r + 1) * HD, at:at + STACK].rearrange("p (h s) -> p h s", s=S)
                        src = parts_d[b, which, part].rearrange("(h d) s -> d h s", d=HD)
                        sp.dma_start(dst, src).then_inc(d_stack, 16)
                at = (b % 2) * 2 * STACK + STACK
                sp.dma_start(stack[MAX_ROW:ROWS, at:at + STACK].rearrange("r (n c) -> r n c", c=P),
                             onesb[0:2, :].unsqueeze(1).to_broadcast([2, STACK // P, P])).then_inc(d_stack, 16)

            sp.wait_ge(d_x[B - 1], 16)
            for k in (0, 1, 2, 3):
                load_piece(k, 0)
            for n in range(N_QK):
                b, m = divmod(n, QK_TILES)
                sp.wait_ge(s_lo, n + 1)
                dst = parts_d[b, m // KT].rearrange("c (m p) s -> p c m s", p=P)[:, :, m % KT, :]
                sp.dma_start(dst, parts[:, n % RING, :, :]).then_inc(d_parts[n % RING], 16)
            load_piece(0, 1)
            load_piece(1, 1)
            load_rows(1)
            for n in range(RING):
                sp.wait_ge(d_parts[n], 16 * ((N_QK - n + RING - 1) // RING))
            load_stack(0)

            def expert(e):
                if before(e, E - 2):
                    load_rows(e + 2)
                if after(e, 0):
                    store_rows(e - 1)
                if before(e, E - 1):
                    load_piece(2, e + 1)
                    load_piece(3, e + 1)
                if before(e, E - 2):
                    load_piece(0, e + 2)
                    load_piece(1, e + 2)

            expert(0)
            with sp.Fori(1, E - 2) as e:
                expert(e)
            expert(E - 2)

            expert(E - 1)

            def load_max(g, hg):
                sp.wait_ge(s_mev, g + 1)
                at = (g // GPB % 2) * 2 * STACK + hg * HG * S
                for r in range(2):
                    dst = stack[MAX_ROW + r:MAX_ROW + r + 1, at:at + HG * S].rearrange("r (c t) -> r c t", t=P)
                    sp.dma_start(dst, mrow[16 * r:16 * r + 16, g % 2, :]).then_inc(d_mrow[g % 2], 16)

            load_max(0, 0)
            store_rows(E - 1)
            for b in range(B):
                for hg in range(GPB):
                    g = GPB * b + hg + 1
                    if g < GROUPS:
                        load_max(g, g % GPB)
                    if g == 1:
                        wait_used(sp, 3, E - 1)
                        sp.wait_ge(d_stack, 16 * STACK_LOADS)
                        load_stack(1)
                    if hg == 3 and b + 2 < B:
                        sp.wait_ge(s_exp, 16 * GPB * (b + 1) + 2)
                        sp.wait_ge(d_stack, 16 * STACK_LOADS * (b + 2))
                        load_stack(b + 2)
                    if hg == 2 and b > 0:
                        sp.wait_ge(s_acc, GPB * b + 2)
                        sp.dma_start(out_tiles[b - 1], acc[:, (b - 1) * TB:b * TB, :]).then_inc(d_out, 16)
            sp.wait_ge(s_acc, GPB * B + 2)
            sp.dma_start(out_tiles[B - 1], acc[:, (B - 1) * TB:, :]).then_inc(d_out, 16)
            sp.wait_ge(d_out, 16 * B)

        @block.gpsimd
        def _(pool):
            pool.memset(ident[:], 0.0).then_inc(s_pool, 1)
            pool.memset(identb[:], 0.0).then_inc(s_pool, 1)
            pool.memset(earlier[:], 1.0).then_inc(s_pool, 1)
            pool.wait_ge(s_pool, 3)
            for m in (ident, identb):
                pool.affine_select(out=m[:], in_=m[:], compare_op=ALU.not_equal, fill=1.0, base=0,
                                   pattern=[[-1, P]], channel_multiplier=1).then_inc(s_const, 1)
            pool.affine_select(out=earlier[:], in_=earlier[:], compare_op=ALU.is_gt, fill=0.0, base=0,
                               pattern=[[1, P]], channel_multiplier=-1).then_inc(s_const, 1)
            pool.memset(onesb[:], 1.0).then_inc(s_const, 1)
            pool.memset(warm[:], 0.0).then_inc(s_warm, 1)
            pool.memset(zeros[:], 0.0).then_inc(s_pool, 1)
            for e in range(E):
                pool.memset(descend[:, e:e + 1], float(E - e)).then_inc(s_const, 1)
                pool.memset(starts[:, e:e + 1], float(e * CAP)).then_inc(s_const, 1)
            pool.iota(m_i[:], [[1, NT * E]], base=0, channel_multiplier=-1).then_inc(s_const, 1)
            pool.iota(dump_i[:], [[P, NT]], base=SLOTS, channel_multiplier=1).then_inc(s_const, 1)
            pool.wait_ge(s_pool, 4)
            pool.wait_ge(d_x[B - 1], 16)
            per = SLOTS // P
            pool.dma_start(xd_d[0:SLOTS, :].rearrange("(p r) d -> p r d", r=per),
                           zeros[:, :].unsqueeze(1).to_broadcast([P, per, D])).then_inc(d_zero, 16)
            pool.wait_ge(s_wTh, 5)
            pool.memset(bvb[:], 1.0).then_inc(s_pool, 1)
            pool.wait_ge(s_pool, 5)
            for kt in range(KT):
                pool.tensor_scalar(bvb[:, kt, :], bvb[:, kt, :], b_cols[:, QK_TILES + kt:QK_TILES + kt + 1], None, ALU.mult).then_inc(s_bvb, 1)
            pool.wait_ge(s_bvb, KT)
            pool.tensor_copy(bvb_h[:], bvb[:]).then_inc(s_bvb, 1)
            pool.wait_ge(s_bvb, KT + 1)
            pool.tensor_tensor(bvb_l[:], bvb[:], bvb_h[:].bitcast(F32), ALU.subtract).then_inc(s_bvb, 1)

            def split_low(k, e):
                pool.wait_ge(w_hi[k], e + 1)
                pool.tensor_tensor(piece(k, wi_l, wo_l), piece(k, raw_wi, raw_wo), piece(k, wi_h, wo_h).bitcast(F32),
                                   ALU.subtract).then_inc(w_lo[k], 1)

            for k in range(4):
                split_low(k, 0)

            pool.wait_ge(d_zero, 16)
            pool.wait_ge(s_index, 1)
            for t in range(NT):
                pool.indirect_dma_start(out=xd_d, out_offset=bass.IndirectOffsetOnAxis(ap=to_slot[:, t:t + 1], axis=0),
                                        in_=xn[:, t, :], in_offset=None).then_inc(d_scatter, 16)

            pool.wait_ge(d_scatter, 16 * NT)
            pool.dma_start(xd[:, 0:2, :], xd_d[0:2 * P, :].rearrange("(t p) d -> p t d", p=P)).then_inc(d_xd0, 16)
            pool.dma_start(xd[0:CAP - 2 * P, 2, :], xd_d[2 * P:CAP, :]).then_inc(d_xd0, 16)

            def expert(e):
                if after(e, 0):
                    split_low(3, e)
                if before(e, E - 1):
                    split_low(2, e + 1)

            def add_bias(b):
                tiles = slice(b * TB, (b + 1) * TB)
                pool.tensor_tensor(acc[:, tiles, :], acc[:, tiles, :], bias[:, :].unsqueeze(1).to_broadcast([P, TB, D]),
                                   ALU.add).then_inc(s_xb, 1)

            def copy_v(pair, u):
                g = 2 * pair + u
                if after(g, 1):
                    pool.wait_ge(s_pv, TB * g - TB)
                src = vg[:, bass.ds(pair // 2 * TB, TB), bass.ds(pair % 2 * 2 * HG * HD + u * HG * HD, HG * HD)]
                pool.tensor_copy(vslot[:, u, :, :, 0:HD], src.rearrange("p t (j c) -> p t j c", j=HG)
                                 ).then_inc(s_vslot, 1)

            expert(0)
            pool.wait_ge(s_qk, N_QK)
            pool.memset(vslot[:], 0.0).then_inc(s_vz, 1)
            pool.wait_ge(s_bias, 1)
            add_bias(0)
            add_bias(1)
            with pool.Fori(1, E - 1) as e:
                expert(e)
            pool.memset(vslot[:, :, :, :, HD:HD + 1], 1.0).then_inc(s_vz, 1)
            add_bias(2)
            expert(E - 1)
            pool.wait_ge(s_vz, 2)
            copy_v(0, 0)
            copy_v(0, 1)
            add_bias(3)

            pool.wait_ge(s_index, 3)
            pool.wait_ge(d_y, 32 * E)

            def gather(b):
                for t in range(b * TB, (b + 1) * TB):
                    pool.indirect_dma_start(out=y_tok[:, t, :], out_offset=None, in_=yd_d,
                                            in_offset=bass.IndirectOffsetOnAxis(ap=from_slot[:, t:t + 1], axis=0)
                                            ).then_inc(d_gather[b], 16)

            pool.wait_ge(s_xb, B)
            gather(0)
            for b in range(B):
                if b + 1 < B:
                    gather(b + 1)
                tiles = slice(b * TB, (b + 1) * TB)
                pool.wait_ge(d_gather[b], 16 * TB)
                pool.tensor_tensor(y_tok[:, tiles, :], y_tok[:, tiles, :],
                                   weight[:, tiles].unsqueeze(2).to_broadcast([P, TB, D]), ALU.mult).then_inc(s_wy, 1)
                pool.wait_ge(s_wy, b + 1)
                pool.tensor_tensor(acc[:, tiles, :], acc[:, tiles, :], y_tok[:, tiles, :], ALU.add).then_inc(s_comb, 1)
                if b == 0:
                    copy_v(1, 0)
                    copy_v(1, 1)
            with pool.Fori(2, PAIRS) as p:
                copy_v(p, 0)
                copy_v(p, 1)

        @block.scalar
        def _(act):
            act.dma_start(w_rows[:], wqkv_in.rearrange("(m p) d -> p m d", p=P)).then_inc(d_w, 16)
            act.dma_start(wo_rows[:], wo_in.rearrange("(m p) d -> p m d", p=P)).then_inc(d_w, 16)
            act.dma_start(gate_rows[:], gate_in).then_inc(d_w, 16)
            act.dma_start(b_rows[:], bqkv_in.rearrange("(m p) -> m p", p=P)).then_inc(d_w, 16)
            act.dma_start(bias[:], bo_in.rearrange("(a d) -> a d", a=1).to_broadcast([P, D])).then_inc(d_small, 16)

            def weight_banks():
                for kt in range(KT):
                    yield wT_h[:, kt, 512:512 + VG], ps[:, 4 + kt, 0:VG]
                for kt in range(KT):
                    yield wT_h[:, kt, 0:512], ps[:, 2 + kt, :]
                yield b_cols[:], ps[:, 7, 0:3 * KT]

            def root(b):
                act.wait_ge(s_var, b + 1)
                act.activation(vare[:, b, :], vare[:, b, :], ACT.Sqrt).then_inc(s_root, 1)

            act.wait_ge(s_warm, 1)
            root(0)
            root(1)
            for n, (dst, src) in enumerate(weight_banks()):
                act.wait_ge(s_wT, n + 1)
                act.activation(dst, src, ACT.Copy).then_inc(s_wTh, 1)

            def split_high(k, e):
                act.wait_ge(d_raw[k], 16 * e + 16)
                if after(e, 0):
                    wait_used(act, k, e - 1)
                act.activation(piece(k, wi_h, wo_h), piece(k, raw_wi, raw_wo), ACT.Copy).then_inc(w_hi[k], 1)

            def tokens_high(b):
                act.wait_ge(s_xT, b + 1)
                act.activation(xT_h[:, b, :, :], ps[:, XT_BANKS[b % 2]:XT_BANKS[b % 2] + 2, :], ACT.Copy).then_inc(s_xTh, 1)

            tokens_high(0)
            tokens_high(1)
            root(2)
            for t in range(NT):
                act.wait_ge(s_v, t + 1)
                act.activation(vg[:, t, :], ps[:, 6 + t % 2, 0:VG], ACT.Copy).then_inc(s_vg, 1)
                if t == TB - 1:
                    act.wait_ge(s_wT, 6)
                    act.activation(woT_h[:], ps[:, 2, :].rearrange("p (k d) -> p k d", k=KT), ACT.Copy).then_inc(s_wTh, 1)
                if t in (TB + 1, 2 * TB + 1):
                    tokens_high(t // TB + 1)
                if t == TB + 1:
                    root(3)
                if t in (TB - 1, TB, 2 * TB - 1, 3 * TB - 1):
                    split_high((TB - 1, TB, 2 * TB - 1, 3 * TB - 1).index(t), 0)
            act.wait_ge(s_wTh, 6)

            def middle_part(n):
                act.wait_ge(s_r, n + 1)
                act.activation(parts[:, n % RING, 1, :], qkr[:, n % 2, :], ACT.Copy).then_inc(s_mid, 1)

            for n in range(N_QK):
                act.wait_ge(s_qk, n + 1)
                if n >= 2:
                    act.wait_ge(s_r, n - 1)
                if n % 2:
                    if n >= RING:
                        act.wait_ge(d_parts[n % RING], 16 * (n // RING))
                    act.activation(parts[:, n % RING, 0, :], ps[:, 4 + n % 2, :], ACT.Identity,
                                   bias=b_cols[:, n % QK_TILES:n % QK_TILES + 1]).then_inc(s_hi_odd, 1)
                act.activation(qkf[:, n % 2, :], ps[:, 4 + n % 2, :], ACT.Identity,
                               bias=b_cols[:, n % QK_TILES:n % QK_TILES + 1]).then_inc(s_qkf, 1)
                if n:
                    middle_part(n - 1)
            middle_part(N_QK - 1)
            act.wait_ge(s_route, 2)
            act.activation(t_b[:], t_a[:], ACT.Exp).then_inc(s_exp8, 1)

            def rows_high(e):
                act.wait_ge(s_xdT, e + 1)
                if after(e, 0):
                    wait_used(act, 1, e - 1)
                act.activation(xdT_h[:], ps[:, 4:6, 0:CAP], ACT.Copy).then_inc(s_xdh, 1)

            def turn_max(g, u):
                act.wait_ge(s_mT, g + 1)
                act.activation(mrow[:, u, :], ps[0:32, 7, 0:P // 2].bitcast(BF16), ACT.Copy).then_inc(s_mev, 1)

            def gelu(e, i):
                n = FT * e + i
                act.wait_ge(s_h, n + 1)
                if after(n, 1):
                    act.wait_ge(s_gl, n - 1)
                act.activation(g32[:, i % 2, :], ps[:, i % 2, 0:CAP], ACT.Gelu).then_inc(s_gelu, 1)

            def expert(e):
                for i in range(FT):
                    gelu(e, i)
                    if i == 1 and after(e, 0):
                        split_high(3, e)
                    if i == 5 and before(e, E - 1):
                        split_high(0, e + 1)
                if before(e, E - 1):
                    rows_high(e + 1)
                    split_high(1, e + 1)
                    split_high(2, e + 1)
                else:
                    turn_max(0, 0)
                    act.activation(warm[:], warm[:], ACT.Exp)
                act.wait_ge(s_y, e + 1)
                if after(e, 0):
                    act.wait_ge(s_yb, e)
                act.activation(yT[:], ps[:, 2:4, 0:CAP], ACT.Copy).then_inc(s_yT, 1)

            act.activation(warm[:], warm[:], ACT.Gelu)
            rows_high(0)
            expert(0)
            with act.Fori(1, E - 1) as e:
                expert(e)
            expert(E - 1)

            def take_out(g, u):
                act.wait_ge(s_pv, TB * g + TB)
                if after(g, 1):
                    act.wait_ge(s_pt, g - 1)
                act.activation(poT[:, u, :], ps[:, 6, :], ACT.Copy).then_inc(s_po, 1)

            def context_high(q):
                act.wait_ge(s_cT, q + 1)
                act.activation(ctxT_h[:], ps[:, 7, :], ACT.Copy).then_inc(s_cTh, 1)

            def group(p, u):
                g = 2 * p + u
                for st in range(TB):
                    if after(g, 0):
                        act.wait_ge(s_pv, TB * g + st + 1 - TB)
                    for j in range(HG):
                        n = 16 * g + HG * st + j
                        act.wait_ge(s_st, n + 1)
                        act.activation(probs[:, st, j, :], ps[:, 4 + j % 2, :], ACT.Exp, scale=SCALE
                                       ).then_inc(s_exp, 1)
                    if st == 0 and after(g, 0):
                        take_out(g - 1, 1 - u)
                    if st == 1 and (u == 0 or before(p, PAIRS - 1)):
                        turn_max(g + 1, 1 - u)
                if u == 0 and after(p, 0):
                    context_high(p - 1)

            act.sem_inc(s_exp, 2)
            act.wait_ge(s_gl, FT * E)
            wait_used(act, 3, E - 1)
            group(0, 0)
            group(0, 1)
            with act.Fori(1, PAIRS - 1) as p:
                group(p, 0)
                group(p, 1)
            group(PAIRS - 1, 0)
            group(PAIRS - 1, 1)
            take_out(GROUPS - 1, 1)
            context_high(PAIRS - 1)

        @block.vector
        def _(dve):
            ln, route = [0], [0]

            def chain(counter, semaphore, instruction):
                instruction.then_inc(semaphore, 1)
                counter[0] += 1
                dve.wait_ge(semaphore, counter[0])

            def statistics(b):
                dve.wait_ge(d_x[b], 16)
                for t in range(TB):
                    last = dve.bn_stats(stats[:, t, :], acc[:, b * TB + t, :])
                chain(ln, s_ln, last)
                for t in range(TB):
                    last = dve.bn_aggr(mv[:, b, t, :], stats[:, t, :])
                chain(ln, s_ln, last)
                dve.tensor_scalar(vare[:, b, :], mv[:, b, :, 1], EPS, None, ALU.add).then_inc(s_var, 1)

            def normalise_tokens(b):
                dve.wait_ge(s_root, b + 1)
                chain(ln, s_ln, dve.reciprocal(rstd[:, b, :], vare[:, b, :]))
                for t in range(TB):
                    last = dve.tensor_scalar(xn[:, b * TB + t, :], acc[:, b * TB + t, :], mv[:, b, t, 0:1],
                                             rstd[:, b, t:t + 1], ALU.subtract, ALU.mult)
                last.then_inc(s_xn, 1)

            def weight_banks():
                for kt in range(KT):
                    yield wT_l[:, kt, 512:512 + VG], ps[:, 4 + kt, 0:VG], wT_h[:, kt, 512:512 + VG]
                for kt in range(KT):
                    yield wT_l[:, kt, 0:512], ps[:, 2 + kt, :], wT_h[:, kt, 0:512]

            dve.wait_ge(s_const, 4 + 2 * E + 2)
            dve.tensor_scalar(m_low[:], m_i[:], E - 1, None, ALU.bitwise_and).then_inc(s_mask, 1)
            dve.tensor_scalar(m_later[:], m_i[:], 0.0, None, ALU.is_gt).then_inc(s_mask, 1)
            dve.wait_ge(s_mask, 2)
            dve.tensor_scalar(m_same[:], m_low[:], 0.0, None, ALU.is_equal).then_inc(s_mask, 1)
            dve.tensor_copy(dump[:], dump_i[:]).then_inc(s_mask, 1)
            dve.wait_ge(s_mask, 4)
            dve.tensor_tensor(tiles_before[:], m_same[:], m_later[:], ALU.mult).then_inc(s_mask, 1)
            statistics(0)
            statistics(1)
            normalise_tokens(0)
            banks = list(weight_banks())

            def weights_low(n):
                dst, src, high = banks[n]
                dve.wait_ge(s_wTh, n + 1)
                dve.tensor_tensor(dst, src, high.bitcast(F32), ALU.subtract).then_inc(s_wTl, 1)

            weights_low(0)
            weights_low(1)
            normalise_tokens(1)

            def tokens_low(b):
                dve.wait_ge(s_xTh, b + 1)
                dve.tensor_tensor(xT_l[:, b, :, :], ps[:, XT_BANKS[b % 2]:XT_BANKS[b % 2] + 2, :],
                                  xT_h[:, b, :, :].bitcast(F32), ALU.subtract).then_inc(s_xTl, 1)

            tokens_low(0)
            statistics(2)
            tokens_low(1)
            weights_low(2)
            weights_low(3)
            normalise_tokens(2)
            statistics(3)
            tokens_low(2)
            normalise_tokens(3)
            dve.wait_ge(s_wTh, 6)
            dve.tensor_tensor(woT_l[:], ps[:, 2, :].rearrange("p (k d) -> p k d", k=KT), woT_h[:].bitcast(F32),
                              ALU.subtract).then_inc(s_wTl, 1)
            tokens_low(3)
            def per_tile(column):
                return column[:].unsqueeze(2).to_broadcast([P, NT, E])

            def per_expert(row):
                return row[:, :].unsqueeze(1).to_broadcast([P, NT, E])

            dve.wait_ge(s_vg, NT)
            logits = vg[:, :, D:D + E]
            chain(route, s_route, dve.tensor_reduce(c_a[:], logits, AX_X, ALU.max))
            chain(route, s_route, dve.tensor_tensor(t_a[:], logits, per_tile(c_a), ALU.subtract))
            chain(route, s_route, dve.scalar_tensor_tensor(out=t_c[:], in0=t_a[:], scalar=0.0, in1=per_expert(descend),
                                                           op0=ALU.is_equal, op1=ALU.mult))
            chain(route, s_route, dve.tensor_reduce(c_b[:], t_c[:], AX_X, ALU.max))
            dve.tensor_tensor(onehb[:], t_c[:], per_tile(c_b), ALU.is_equal).then_inc(s_oneh, 1)
            dve.wait_ge(s_count, 1)
            dve.tensor_copy(countsb[:], ps[:, 6, 256:256 + P]).then_inc(s_countb, 1)
            chain(route, s_route, dve.tensor_tensor(t_c[:], onehb[:], per_expert(starts), ALU.mult))
            chain(route, s_route, dve.tensor_reduce(c_c[:], t_c[:], AX_X, ALU.add))
            dve.wait_ge(s_rank, 1)
            ranks = ps[:, 6, 0:NT * E].rearrange("p (t e) -> p t e", e=E)
            chain(route, s_route, dve.tensor_tensor(t_c[:], ranks, onehb[:], ALU.mult))
            chain(route, s_route, dve.tensor_reduce(c_b[:], t_c[:], AX_X, ALU.add))
            chain(route, s_route, dve.tensor_tensor(c_c[:], c_c[:], c_b[:], ALU.add))
            chain(route, s_route, dve.tensor_tensor(c_d[:], c_c[:], dump[:], ALU.subtract))
            chain(route, s_route, dve.scalar_tensor_tensor(out=c_d[:], in0=c_b[:], scalar=float(CAP), in1=c_d[:],
                                                           op0=ALU.is_lt, op1=ALU.mult))
            dve.tensor_tensor(to_slot[:], c_d[:], dump[:], ALU.add).then_inc(s_index, 1)

            def weights_of_tokens():
                chain(route, s_route, dve.tensor_scalar(keep[:], c_b[:], float(CAP), None, ALU.is_lt))
                dve.tensor_tensor(from_slot[:], c_c[:], keep[:], ALU.mult).then_inc(s_index, 1)
                dve.wait_ge(s_exp8, 1)
                chain(route, s_route, dve.tensor_reduce(c_a[:], t_b[:], AX_X, ALU.add))
                chain(route, s_route, dve.reciprocal(weight[:], c_a[:]))
                dve.tensor_tensor(weight[:], weight[:], keep[:], ALU.mult).then_inc(s_index, 1)

            def split_low(k, e):
                dve.wait_ge(w_hi[k], e + 1)
                dve.tensor_tensor(piece(k, wi_l, wo_l), piece(k, raw_wi, raw_wo), piece(k, wi_h, wo_h).bitcast(F32),
                                  ALU.subtract).then_inc(w_lo[k], 1)

            def low_part(n):
                dve.wait_ge(s_mid, n + 1)
                dve.tensor_tensor(parts[:, n % RING, 2, :], qkr[:, n % 2, :], parts[:, n % RING, 1, :], ALU.subtract
                                  ).then_inc(s_lo, 1)

            for n in range(N_QK):
                dve.wait_ge(s_qkf, n + 1)
                if n % 2 == 0:
                    if n >= RING:
                        dve.wait_ge(d_parts[n % RING], 16 * (n // RING))
                    dve.tensor_copy(parts[:, n % RING, 0, :], qkf[:, n % 2, :]).then_inc(s_hi_even, 1)
                dve.wait_ge(s_hi_odd if n % 2 else s_hi_even, n // 2 + 1)
                if n >= 2:
                    dve.wait_ge(s_lo, n - 1)
                dve.tensor_tensor(qkr[:, n % 2, :], qkf[:, n % 2, :], parts[:, n % RING, 0, :], ALU.subtract
                                  ).then_inc(s_r, 1)
                if n:
                    low_part(n - 1)
            low_part(N_QK - 1)
            weights_of_tokens()
            dve.wait_ge(s_bvp, 1)
            dve.wait_ge(d_small, 16 * LOADS_SMALL)
            dve.tensor_tensor(bias[:], ps[:, 7, 0:D], bias[:], ALU.add).then_inc(s_bias, 1)

            def reduce_max(g, u, c):
                dve.wait_ge(s_smax, 8 * g + c + 1)
                col = c // 2 * TB + c % 2 * 2
                dve.tensor_reduce(negm[:, u, col:col + 2], ps[:, 2 * (c % 2):2 * (c % 2) + 2, :], AX_X, ALU.max,
                                  negate=True).then_inc(s_red, 1)

            def split_max(g, u):
                dve.wait_ge(s_red, 8 * g + 8)
                if after(g, 1):
                    dve.wait_ge(s_mT, g - 1)
                dve.tensor_copy(mpart[:, u, 0, :], negm[:, u, :]).then_inc(s_mhi, 1)
                dve.wait_ge(s_mhi, g + 1)
                dve.tensor_tensor(mpart[:, u, 1, :], negm[:, u, :], mpart[:, u, 0, :], ALU.subtract
                                  ).then_inc(s_msplit, 1)

            def first_max(e, half):
                dve.wait_ge(s_smax, 2 * e + half + 1)
                dve.tensor_reduce(negm[:].rearrange("p u c -> p (u c)")[:, bass.ds(e * TB + 2 * half, 2)], ps[:, 4:6, :], AX_X, ALU.max, negate=True
                                  ).then_inc(s_red, 1)

            def rows_low(e):
                dve.wait_ge(s_xdh, e + 1)
                dve.tensor_tensor(xdT_l[:], ps[:, 4:6, 0:CAP], xdT_h[:].bitcast(F32), ALU.subtract
                                  ).then_inc(s_xdl, 1)

            def rows_back(e):
                dve.wait_ge(s_yb, e + 1)
                if after(e, 0):
                    dve.wait_ge(d_y, 32 * e)
                dve.tensor_copy(y_rows[:, 0:2, :], ps[:, 6, :].rearrange("p (t d) -> p t d", d=D)).then_inc(s_yr, 1)
                dve.tensor_copy(y_rows[0:CAP - 2 * P, 2, :], ps[0:CAP - 2 * P, 7, 0:D]).then_inc(s_yr, 1)

            def expert(e):
                for i in range(FT):
                    n = FT * e + i
                    dve.wait_ge(s_gelu, n + 1)
                    if i % HALF == 0 and after(e, 0):
                        wait_used(dve, 2 + i // HALF, e - 1)
                    dve.tensor_copy(gh[:, i, :], g32[:, i % 2, :]).then_inc(s_gh, 1)
                    dve.wait_ge(s_gh, n + 1)
                    dve.tensor_tensor(gl[:, i, :], g32[:, i % 2, :], gh[:, i, :].bitcast(F32), ALU.subtract
                                      ).then_inc(s_gl, 1)
                    if i == 3 and after(e, 0):
                        rows_back(e - 1)
                    if i == 6 and before(e, E - 1):
                        split_low(0, e + 1)
                if before(e, E - 1):
                    rows_low(e + 1)
                    split_low(1, e + 1)
                first_max(e, 0)
                first_max(e, 1)

            rows_low(0)
            for n in range(RING):
                dve.wait_ge(d_parts[n], 16 * (N_QK // RING))
            expert(0)
            with dve.Fori(1, E - 1) as e:
                expert(e)
            split_max(0, 0)
            expert(E - 1)

            dve.sem_inc(s_acc, 2)

            def normalise(g, u):
                dve.wait_ge(s_pt, g + 1)
                rows = ps[:, 7, :].rearrange("p (i j c) -> p i j c", i=TB, j=HG)
                dve.reciprocal(rsum[:, u], rows[:, :, :, HD]).then_inc(s_rs, 1)
                dve.wait_ge(s_rs, g + 1)
                dst = ctx_sb[:, :, u * HG * HD:(u + 1) * HG * HD].rearrange("p i (j c) -> p i j c", j=HG)
                dve.tensor_tensor(dst, rows[:, :, :, 0:HD], rsum[:, u].unsqueeze(3).to_broadcast([P, TB, HG, HD]),
                                  ALU.mult).then_inc(s_ctx, 1)

            def context_low(q):
                dve.wait_ge(s_cTh, q + 1)
                dve.tensor_tensor(ctxT_l[:], ps[:, 7, :], ctxT_h[:].bitcast(F32), ALU.subtract).then_inc(s_cTl, 1)

            def accumulate(q, half):
                dve.wait_ge(s_op, 2 * q + half + 1)
                dve.wait_ge(s_comb, q // 2 + 1)
                tiles = acc[:, bass.ds(q // 2 * TB + 2 * half, 2), :]
                dve.tensor_tensor(tiles, ps[:, 7, :].rearrange("p (i d) -> p i d", i=2), tiles, ALU.add
                                  ).then_inc(s_acc, 1)

            def group(p, u):
                g = 2 * p + u
                more = before(p, PAIRS - 1)
                for st in range(TB):
                    if more:
                        reduce_max(g + 2, u, 2 * st)
                        reduce_max(g + 2, u, 2 * st + 1)
                    if st == 0 and not after(g, 0):
                        rows_back(E - 1)
                    if st == 0 and u == 1 and after(p, 0):
                        accumulate(p - 1, 0)
                    if st == 2 and after(g, 0):
                        normalise(g - 1, 1 - u)
                if more:
                    split_max(g + 2, u)
                if u == 0 and after(p, 0):
                    context_low(p - 1)
                if u == 1 and after(p, 0):
                    accumulate(p - 1, 1)

            split_max(1, 1)
            group(0, 0)
            group(0, 1)
            with dve.Fori(1, PAIRS - 1) as p:
                group(p, 0)
                group(p, 1)
            group(PAIRS - 1, 0)
            group(PAIRS - 1, 1)
            normalise(GROUPS - 1, 1)
            context_low(PAIRS - 1)
            accumulate(PAIRS - 1, 0)
            accumulate(PAIRS - 1, 1)

        @block.tensor
        def _(pe):
            pe.wait_ge(s_const, 4)

            def keep_warm(products, bank):
                for _ in range(products):
                    pe.matmul(ps[:, bank, 0:P], onesb[:], onesb[:], start=True, stop=True)

            keep_warm(48, 0)

            def turn(dst, src, identity):
                return pe.transpose(dst, src, identity)

            def product(dst, w_parts, x_parts, first, last):
                (wh, wl), (xh, xl) = w_parts, x_parts
                pe.matmul(dst, wh, xh, start=first, stop=False)
                pe.matmul(dst, wl, xh, start=False, stop=False)
                return pe.matmul(dst, wh, xl, start=False, stop=last)

            pe.wait_ge(d_w, 16 * LOADS_W)
            for kt in range(KT):
                k = slice(kt * P, (kt + 1) * P)
                for m in range(2):
                    turn(ps[:, 4 + kt, m * P:(m + 1) * P], w_rows[:, 4 + m, k], ident[:])
                turn(ps[:, 4 + kt, 2 * P:2 * P + E], gate_rows[:, k], ident[0:E, 0:E]).then_inc(s_wT, 1)
            for kt in range(KT):
                k = slice(kt * P, (kt + 1) * P)
                for m in range(4):
                    last = turn(ps[:, 2 + kt, m * P:(m + 1) * P], w_rows[:, m, k], ident[:])
                last.then_inc(s_wT, 1)
            turn(ps[:, 7, 0:3 * KT], b_rows[:], ident[0:3 * KT, 0:3 * KT]).then_inc(s_wT, 1)

            def turn_output_weights():
                pe.wait_ge(s_wTl, 3)
                for kt in range(KT):
                    for m in range(KT):
                        last = turn(ps[:, 2, kt * D + m * P:kt * D + (m + 1) * P], wo_rows[:, m, kt * P:(kt + 1) * P], ident[:])
                last.then_inc(s_wT, 1)

            def turn_tokens(b):
                pe.wait_ge(s_xn, b + 1)
                if b >= 2:
                    pe.wait_ge(s_xTl, b - 1)
                for kt in range(KT):
                    for t in range(TB):
                        last = turn(ps[:, XT_BANKS[b % 2] + kt, t * P:(t + 1) * P], xn[:, b * TB + t, kt * P:(kt + 1) * P], ident[:])
                last.then_inc(s_xT, 1)

            turn_tokens(0)
            keep_warm(24, 6)
            pe.wait_ge(s_wTl, 2)
            turn_tokens(1)
            pe.wait_ge(s_wTh, 5)
            for b in range(B):
                pe.wait_ge(s_xTl, b + 1)
                for i in range(TB):
                    t = b * TB + i
                    if i == 2 and b and b + 1 < B:
                        turn_tokens(b + 1)
                    if t >= 2:
                        pe.wait_ge(s_vg, t - 1)
                    for kt in range(KT):
                        col = slice(i * P, (i + 1) * P)
                        last = product(ps[:, 6 + t % 2, 0:VG], (xT_h[:, b, kt, col], xT_l[:, b, kt, col]),
                                       (wT_h[:, kt, 2 * D:], wT_l[:, kt, 2 * D:]), kt == 0, kt == KT - 1)
                    last.then_inc(s_v, 1)
                if b == 0:
                    turn_output_weights()

            def project_bias():
                pe.wait_ge(s_vg, NT)
                pe.wait_ge(s_wTl, 5)
                pe.wait_ge(s_bvb, KT + 2)
                for kt in range(KT):
                    last = product(ps[:, 7, 0:D], (bvb_h[:, kt, :], bvb_l[:, kt, :]),
                                   (woT_h[:, kt, :], woT_l[:, kt, :]), kt == 0, kt == KT - 1)
                last.then_inc(s_bvp, 1)

            hot = onehb[:].rearrange("p t e -> p (t e)")

            def count():
                pe.wait_ge(s_oneh, 1)
                pe.matmul(ps[:, 6, 256:256 + P], hot, onesb[:], start=True, stop=True).then_inc(s_count, 1)

            def rank():
                pe.wait_ge(s_countb, 1)
                pe.wait_ge(s_mask, 5)
                pe.matmul(ps[:, 6, 0:NT * E], earlier[:], hot, start=True, stop=False)
                pe.matmul(ps[:, 6, 0:NT * E], countsb[:], tiles_before[:], start=False, stop=True).then_inc(s_rank, 1)

            for n in range(N_QK):
                b, m = divmod(n, QK_TILES)
                if n == 1:
                    pe.wait_ge(s_wTl, 4)
                    count()
                if n == 4:
                    project_bias()
                if n == 2:
                    rank()
                if n >= 2:
                    pe.wait_ge(s_qkf, n - 1)
                elif n == 0:
                    pe.wait_ge(s_xTl, B)
                for kt in range(KT):
                    col = slice(m * P, (m + 1) * P)
                    last = product(ps[:, 4 + n % 2, :], (wT_h[:, kt, col], wT_l[:, kt, col]),
                                   (xT_h[:, b, kt, :], xT_l[:, b, kt, :]), kt == 0, kt == KT - 1)
                last.then_inc(s_qk, 1)

            def turn_max(g, u):
                pe.wait_ge(s_msplit, g + 1)
                turn(ps[0:2 * HG * TB, 7, 0:P // 2].bitcast(BF16), mpart[:, u].rearrange("p r c -> p (r c)"), identb[:]
                     ).then_inc(s_mT, 1)

            def first_max(e, half):
                if half:
                    pe.wait_ge(s_red, 2 * e + 1)
                elif before(e, E - 1):
                    pe.wait_ge(s_xdl, e + 2)
                for i in range(2):
                    last = pe.matmul(ps[:, 4 + i, :], stack[0:MAX_ROW, bass.ds(e * S + (2 * half + i) * P, P)],
                                     stack[0:MAX_ROW, bass.ds(e * S + STACK, S)], start=True, stop=True)
                last.then_inc(s_smax, 1)

            def turn_rows(e):
                if after(e, 0):
                    pe.wait_ge(d_xd, 32 * e)
                else:
                    pe.wait_ge(d_xd0, 32)
                if after(e, 1):
                    pe.wait_ge(s_red, 2 * e - 2)
                elif after(e, 0):
                    pe.wait_ge(s_xdl, 1)
                for kt in range(KT):
                    for r, (at, rows) in enumerate(ROW_TILES):
                        last = turn(ps[:, 4 + kt, at:at + rows], xd[0:rows, r, kt * P:(kt + 1) * P], ident[0:rows, 0:rows])
                last.then_inc(s_xdT, 1)

            def turn_back(e):
                pe.wait_ge(s_yT, e + 1)
                if after(e, 0):
                    pe.wait_ge(s_yr, 2 * e)
                for r, (at, rows) in enumerate(ROW_TILES):
                    for kt in range(KT):
                        to = r % 2 * D + kt * P
                        last = turn(ps[0:rows, 6 + r // 2, to:to + P], yT[:, kt, at:at + rows], ident[:])
                last.then_inc(s_yb, 1)

            def expert(e):
                for i in range(FT):
                    n = FT * e + i
                    if i % HALF == 0:
                        pe.wait_ge(w_lo[i // HALF], e + 1)
                    if i == 0:
                        pe.wait_ge(s_xdl, e + 1)
                    if after(n, 1):
                        pe.wait_ge(s_gelu, n - 1)
                    for kt in range(KT):
                        col = slice(i * P, (i + 1) * P)
                        last = product(ps[:, i % 2, 0:CAP], (wi_h[:, kt, col], wi_l[:, kt, col]),
                                       (xdT_h[:, kt, :], xdT_l[:, kt, :]), kt == 0, kt == KT - 1)
                    last.then_inc(s_h, 1)
                    if i == 6 and not before(e, E - 1):
                        pe.wait_ge(s_yr, 2 * E - 2)
                        turn_max(0, 0)
                    if i == 2 and after(e, 0):
                        turn_back(e - 1)
                    if i == 5 and before(e, E - 1):
                        turn_rows(e + 1)
                if after(e, 0):
                    pe.wait_ge(s_yT, e)
                for i in range(FT):
                    if i % HALF == 0:
                        pe.wait_ge(w_lo[2 + i // HALF], e + 1)
                    pe.wait_ge(s_gl, FT * e + i + 1)
                    for m in range(KT):
                        col = slice(m * P, (m + 1) * P)
                        last = product(ps[:, 2 + m, 0:CAP], (wo_h[:, i, col], wo_l[:, i, col]),
                                       (gh[:, i, :], gl[:, i, :]), i == 0, i == FT - 1)
                    if i == HALF - 1:
                        last.then_inc(s_yhalf, 1)
                    if i == FT - 1:
                        last.then_inc(s_y, 1)
                    if i in ((4, 7) if before(e, E - 1) else (1, 4)):
                        if not after(e, 0) and i == 4:
                            pe.wait_ge(d_stack, 16 * STACK_LOADS)
                        first_max(e, int(i == (7 if before(e, E - 1) else 4)))

            pe.wait_ge(s_qkf, N_QK)
            keep_warm(56, 0)
            turn_rows(0)
            expert(0)
            with pe.Fori(1, E - 1) as e:
                expert(e)
            expert(E - 1)
            pe.wait_ge(s_gelu, FT * E)
            pe.wait_ge(s_yT, E)
            pe.wait_ge(s_red, 2 * E)
            pe.wait_ge(s_mev, 1)
            woT_hf, woT_lf = (m[:].rearrange("p k d -> p (k d)") for m in (woT_h, woT_l))

            def max_scores(p, u, c):
                n = 8 * (2 * p + u) + c
                if after(n, 1):
                    pe.wait_ge(s_red, n - 1)
                at = (u * HG + c // 2) * S
                for i in range(2):
                    col = at + (c % 2 * 2 + i) * P
                    last = pe.matmul(ps[:, 2 * (c % 2) + i, :], stack[0:MAX_ROW, bass.ds(stack_at(p, False) + col, P)],
                                     stack[0:MAX_ROW, bass.ds(stack_at(p, True) + at, S)], start=True, stop=True)
                last.then_inc(s_smax, 1)

            def scores(p, u, st, j):
                n = 16 * (2 * p + u) + HG * st + j
                pe.wait_ge(s_exp, n + 1)
                at = (u * HG + j) * S
                pe.matmul(ps[:, 4 + j % 2, :], stack[0:ROWS, bass.ds(stack_at(p, True) + at + st * P, P)],
                          stack[0:ROWS, bass.ds(stack_at(p, False) + at, S)], start=True, stop=True).then_inc(s_st, 1)

            def weigh(g, u, st, half):
                if st == 0 and half:
                    return
                pe.wait_ge(s_exp, 16 * g + HG * st + HG + 2)
                if st == 0:
                    pe.wait_ge(s_vslot, g + 1)
                    if after(g, 0):
                        pe.wait_ge(s_po, g)
                    else:
                        pe.wait_ge(s_yr, 2 * E)
                col = slice(half * S // 2, (half + 1) * S // 2) if st else slice(0, S)
                for j in range(HG):
                    last = pe.matmul(ps[32 * j:32 * j + 32, 6, col], vslot[:, u, st, j, :], probs[:, st, j, col],
                                     start=(st == 0), stop=(st == TB - 1 and half == 1))
                if half or st == 0:
                    last.then_inc(s_pv, 1)

            def turn_out(g, u):
                pe.wait_ge(s_po, g + 1)
                for i in range(TB):
                    last = turn(ps[:, 7, i * P:(i + 1) * P], poT[:, u, i * P:(i + 1) * P], ident[:])
                last.then_inc(s_pt, 1)

            def turn_context(q):
                pe.wait_ge(s_ctx, 2 * q + 2)
                for i in range(TB):
                    last = turn(ps[:, 7, i * P:(i + 1) * P], ctx_sb[:, i, :], ident[:])
                last.then_inc(s_cT, 1)

            def project(q, half):
                rows = bass.ds(q % 2 * D, D)
                for i in range(2):
                    col = slice((2 * half + i) * P, (2 * half + i + 1) * P)
                    last = product(ps[:, 7, i * D:(i + 1) * D], (ctxT_h[:, col], ctxT_l[:, col]),
                                   (woT_hf[:, rows], woT_lf[:, rows]), True, True)
                last.then_inc(s_op, 1)

            def group(p, u):
                g = 2 * p + u
                more = before(p, PAIRS - 1)
                if more and u == 0:
                    pe.wait_ge(d_stack, 16 * STACK_LOADS * ((p + 1) // 2 + 1))
                pe.wait_ge(d_mrow[u], 32 * p + 32)
                for st in range(TB):
                    for j in range(HG):
                        scores(p, u, st, j)
                        if j % 2 == 0:
                            if more:
                                max_scores(p + 1, u, 2 * st + j // 2)
                        elif st:
                            weigh(g, u, st - 1, j // 2)
                        elif after(g, 0):
                            weigh(g - 1, 1 - u, TB - 1, j // 2)
                        elif j == 1:
                            turn_back(E - 1)
                    if st == 0 and u == 1 and after(p, 0):
                        pe.wait_ge(s_cTh, p)
                        pe.wait_ge(s_cTl, p)
                        project(p - 1, 0)
                    if st == 1 and (u == 0 or more):
                        pe.wait_ge(s_mev, g + 1)
                        if after(g, 1):
                            pe.wait_ge(s_ctx, g - 1)
                        if after(p, 0):
                            pe.wait_ge(s_acc, 2 * p + u)
                        turn_max(g + 1, 1 - u)
                    if st == 2 and after(g, 0):
                        if u == 0 or more:
                            pe.wait_ge(s_mev, g + 2)
                        else:
                            pe.wait_ge(s_acc, 2 * p + 1)
                        turn_out(g - 1, 1 - u)
                    if st == 3 and u == 0 and after(p, 0):
                        turn_context(p - 1)
                    if st == 3 and u == 1 and after(p, 0):
                        pe.wait_ge(s_ctx, g)
                        project(p - 1, 1)

            group(0, 0)
            group(0, 1)
            with pe.Fori(1, PAIRS - 1) as p:
                group(p, 0)
                group(p, 1)
            group(PAIRS - 1, 0)
            group(PAIRS - 1, 1)
            for half in range(2):
                weigh(GROUPS - 1, 1, TB - 1, half)
            pe.wait_ge(s_acc, 2 * PAIRS)
            turn_out(GROUPS - 1, 1)
            turn_context(PAIRS - 1)
            pe.wait_ge(s_cTh, PAIRS)
            pe.wait_ge(s_cTl, PAIRS)
            project(PAIRS - 1, 0)
            pe.wait_ge(s_acc, 2 * PAIRS + 1)
            project(PAIRS - 1, 1)


_INS = ["L0_attn_hidden_states", "L0_attn_Wqkv_w", "L0_attn_Wqkv_b", "L0_attn_out_w", "L0_attn_out_b",
        "L0_ffn_gate_weight", "L0_ffn_wi", "L0_ffn_wo"]


def kernel(**inputs):
    import numpy as _np
    import concourse.bacc as _bacc
    from concourse import mybir as _mybir
    from concourse.bass_utils import run_bass_kernel_spmd as _run

    nc = _bacc.Bacc("TRN2", target_bir_lowering=False, num_devices=1)
    arrays, args = {}, []
    for name in _INS:
        a = _np.ascontiguousarray(inputs[name])
        arrays[f"in_{name}"] = a
        args.append(nc.dram_tensor(f"in_{name}", a.shape, _mybir.dt.from_np(a.dtype), kind="ExternalInput").ap())
    shape = arrays["in_" + _INS[0]].shape
    args.append(nc.dram_tensor("out_0", shape, _mybir.dt.float32, kind="ExternalOutput").ap())
    transformer_block(nc, *args)
    r = _run(nc, [arrays], core_ids=[0])
    return r.results[0]["out_0"]
```

```python
from contextlib import ExitStack

import concourse.bass as bass
from concourse import mybir

F32 = mybir.dt.float32
F32R = mybir.dt.float32r
BF16 = mybir.dt.bfloat16
I32 = mybir.dt.int32
ALU = mybir.AluOpType
ACT = mybir.ActivationFunctionType
AX_X = mybir.AxisListType.X
P = 128

Q_TERMS = (0, 0, 1, 1, 0, 2)
K_TERMS = (0, 1, 0, 1, 2, 0)


def before(index, limit):
    return index < limit if isinstance(index, int) else True


def after(index, limit):
    return index > limit if isinstance(index, int) else True


def transformer_block(nc, x_in, wqkv_in, bqkv_in, wo_in, bo_in, gate_in, wi_in, wout_in, out):
    B, S, D = x_in.shape
    T = B * S
    NT = T // P
    TB = S // P
    KT = D // P
    H = 16
    HD = D // H
    E, _, FF = wi_in.shape
    CAP = int(1.25 * T / E)
    CAP += CAP % 2
    FT = FF // P
    HALF = FT // 2
    SLOTS = E * CAP
    EPS = 1e-5
    SCALE = float(HD) ** -0.5
    NTERM = len(Q_TERMS)
    MAX_ROW = NTERM * HD
    ROWS = MAX_ROW + 2
    HG = 4
    GROUPS = B * H // HG
    PAIRS = GROUPS // 2
    GPB = H // HG
    ROW_TILES = [(r, min(P, CAP - r)) for r in range(0, CAP, P)]
    VG = D + E
    QK_TILES = 2 * KT
    RING = 8
    ROUTE_TILES = (NT // 2, NT)
    ROUTE_BANK = 3
    ROW_BANKS = (0, 4)
    QKR = 3
    ROWS_AT = 9
    QK_BANKS = (4, 5, 6)
    XT_BANKS = (0, 4)
    STACK = H * S
    assert S == 4 * P and D == 2 * P and FT == 8 and len(ROW_TILES) == 3 and GPB == 4 and HG * HD * 2 == P

    ctx = ExitStack()
    with ctx:
        def sem(name):
            return ctx.enter_context(nc.semaphore(name))

        base = (nc.sbuf_base + 31) // 32 * 32
        ARENA = 206 * 1024
        ctx.enter_context(nc.sbuf_tensor("arena", [P, ARENA // 4], F32))
        cursor = [0]

        def place(name, shape, dtype, at=None):
            size = 2 if dtype == BF16 else 4
            for n in shape[1:]:
                size *= n
            size = (size + 31) // 32 * 32
            offset = cursor[0] if at is None else at
            tensor = nc.alloc_sbuf_tensor_at(name, shape, dtype, offset=base + offset)
            if at is None:
                cursor[0] += size
                assert cursor[0] <= ARENA, (name, cursor[0])
            return tensor, offset + size

        def new(name, shape, dtype):
            return place(name, shape, dtype)[0]

        acc = new("acc", [P, NT, D], F32)
        xn = new("xn", [P, NT, D], F32)
        vg = new("vg", [P, NT, VG], F32)
        woT_h = new("woT_h", [P, KT, D], F32R)
        woT_l = new("woT_l", [P, KT, D], F32R)

        r_stack = cursor[0]
        stack = new("stack", [P, 4 * STACK], BF16)
        xT_h, at = place("xT_h", [P, B, KT, S], F32R, r_stack)
        xT_l, at = place("xT_l", [P, B, KT, S], F32R, at)
        r_second = r_stack + 4 * STACK
        wi_h, at = place("wi_h", [P, KT, FF], F32R, r_second)
        wi_l, at = place("wi_l", [P, KT, FF], F32R, at)
        wo_h, at = place("wo_h", [P, FT, D], F32R, at)
        wo_l, at = place("wo_l", [P, FT, D], F32R, at)
        assert at == r_second + 4 * STACK

        r_probs = cursor[0]
        gh, at = place("gh", [P, FT, CAP], F32R, r_probs)
        gl, end = place("gl", [P, FT, CAP], F32R, at)
        qkr, at = place("qkr", [P, QKR, S], F32, r_probs)
        parts, at = place("parts", [P, RING, 3, S], BF16, at)
        probs, cursor[0] = place("probs", [P, TB, HG, S], F32, r_probs)
        assert max(at, end) <= cursor[0]

        r_weights = cursor[0]
        wT_h = new("wT_h", [P, KT, 2 * D + VG], F32R)
        wT_l = new("wT_l", [P, KT, 2 * D + VG], F32R)
        w_rows = new("w_rows", [P, 3 * KT, D], F32)
        poT, at = place("poT", [P, 2, S], F32, r_weights)
        ctx_sb, at = place("ctx_sb", [P, TB, P], F32, at)
        ctxT_h, at = place("ctxT_h", [P, S], F32R, at)
        ctxT_l, at = place("ctxT_l", [P, S], F32R, at)
        vslot, at = place("vslot", [P, 2, TB, HG, 32], F32, at)
        mrow, at = place("mrow", [32, 2, P], BF16, at)
        negm, at = place("negm", [P, 2, HG * TB], F32, at)
        mpart, at = place("mpart", [P, 2, 2, HG * TB], BF16, at)
        rsum, at = place("rsum", [P, 2, TB, HG], F32, at)
        assert at <= cursor[0]

        raw_wi = new("raw_wi", [P, KT, FF], F32)
        raw_wo = new("raw_wo", [P, FT, D], F32)
        zeros = place("zeros", [P, D], F32, cursor[0])[0]
        xd = new("xd", [P, 3, D], F32)
        gate_rows = place("gate_rows", [E, D], F32, cursor[0])[0]
        xdT_h = new("xdT_h", [P, KT, CAP], F32R)
        xdT_l = new("xdT_l", [P, KT, CAP], F32R)
        wo_rows = place("wo_rows", [P, KT, D], F32, cursor[0])[0]
        g32 = new("g32", [P, 2, CAP], F32)
        r_yT = cursor[0]
        yT = new("yT", [P, KT, CAP], F32)
        t_c, at = place("t_c", [P, NT, E], F32, r_yT)
        assert at <= cursor[0]
        r_rows = cursor[0]
        y_rows = new("y_rows", [P, 3, D], F32)
        bvb, at = place("bvb", [P, KT, P], F32, r_rows)
        bvb_h, at = place("bvb_h", [P, KT, P], F32R, at)
        bvb_l, at = place("bvb_l", [P, KT, P], F32R, at)
        assert at <= cursor[0]

        ident = new("ident", [P, P], F32)
        identb = new("identb", [P, P], BF16)
        earlier = new("earlier", [P, P], BF16)
        onesb = new("onesb", [P, P], BF16)
        tiles_before = new("tiles_before", [P, NT * E], BF16)
        countsb = new("countsb", [P, P], BF16)
        m_i = place("m_i", [P, NT * E], I32, r_probs)[0]
        m_low = place("m_low", [P, NT * E], I32, r_probs + 4 * NT * E)[0]
        m_same = place("m_same", [P, NT * E], F32, r_probs + 8 * NT * E)[0]
        m_later = place("m_later", [P, NT * E], F32, r_probs + 12 * NT * E)[0]
        b_rows = new("b_rows", [3 * KT, P], F32)
        b_cols = new("b_cols", [P, 3 * KT], F32)
        bias = new("bias", [P, D], F32)
        stats = new("stats", [P, TB, 6], F32)
        mv = new("mv", [P, B, TB, 2], F32)
        vare = new("vare", [P, B, TB], F32)
        rstd = new("rstd", [P, B, TB], F32)
        descend = new("descend", [P, E], F32)
        starts = new("starts", [P, E], F32)
        onehb = new("onehb", [P, NT, E], BF16)
        c_a = new("c_a", [P, NT], F32)
        c_b = new("c_b", [P, NT], F32)
        c_c = new("c_c", [P, NT], F32)
        c_d = new("c_d", [P, NT], F32)
        keep = new("keep", [P, NT], F32)
        weight = new("weight", [P, NT], F32)
        dump_i = new("dump_i", [P, NT], I32)
        t_a = new("t_a", [P, NT, E], F32)
        t_b = new("t_b", [P, NT, E], F32)
        warm = new("warm", [P, 1], F32)
        dump = new("dump", [P, NT], F32)
        to_slot = new("to_slot", [P, NT], I32)
        from_slot = new("from_slot", [P, NT], I32)
        y_tok = xn

        ps = ctx.enter_context(nc.psum_tensor("ps", [P, 8, 512], F32))

        parts_d = nc.dram_tensor("parts_scratch", [B, 2, 3, D, S], BF16).ap()
        xd_d = nc.dram_tensor("slots_scratch", [SLOTS + T, D], F32).ap()
        yd_d = nc.dram_tensor("expert_rows_scratch", [SLOTS, D], F32).ap()

        d_x = [sem(f"d_x{b}") for b in range(B)]
        d_w, d_small, d_zero = sem("d_w"), sem("d_small"), sem("d_zero")
        s_const, s_pool, s_warm = sem("s_const"), sem("s_pool"), sem("s_warm")
        s_ln, s_var, s_root, s_xn = sem("s_ln"), sem("s_var"), sem("s_root"), sem("s_xn")
        s_wT, s_wTh, s_wTl = sem("s_wT"), sem("s_wTh"), sem("s_wTl")
        s_xT, s_xTh, s_xTl = sem("s_xT"), sem("s_xTh"), sem("s_xTl")
        s_v, s_vg = sem("s_v"), sem("s_vg")
        s_mask, s_count, s_countb = sem("s_mask"), sem("s_count"), sem("s_countb")
        s_route, s_exp8, s_oneh, s_rank = sem("s_route"), sem("s_exp8"), sem("s_oneh"), sem("s_rank")
        s_index = sem("s_index")
        d_scatter = sem("d_scatter")
        s_bvb, s_bvp, s_bias, s_xb = sem("s_bvb"), sem("s_bvp"), sem("s_bias"), sem("s_xb")
        s_qk, s_hi, s_r, s_mid, s_lo = sem("s_qk"), sem("s_hi"), sem("s_r"), sem("s_mid"), sem("s_lo")
        d_parts = [sem(f"d_parts{n}") for n in range(RING)]
        d_raw = [sem(f"d_raw{k}") for k in range(4)]
        w_hi = [sem(f"w_hi{k}") for k in range(4)]
        w_lo = [sem(f"w_lo{k}") for k in range(4)]
        s_yhalf = sem("s_yhalf")
        d_xd, s_xdT, s_xdh, s_xdl = sem("d_xd"), sem("s_xdT"), sem("s_xdh"), sem("s_xdl")
        s_h, s_gelu, s_gh, s_gl = sem("s_h"), sem("s_gelu"), sem("s_gh"), sem("s_gl")
        s_y, s_yT, s_yb, s_yr, d_y = sem("s_y"), sem("s_yT"), sem("s_yb"), sem("s_yr"), sem("d_y")
        d_gather = [sem(f"d_gather{b}") for b in range(B)]
        s_wy, s_comb = sem("s_wy"), sem("s_comb")
        d_stack = sem("d_stack")
        s_vz, s_vslot = sem("s_vz"), sem("s_vslot")
        s_smax, s_red, s_mhi, s_msplit = sem("s_smax"), sem("s_red"), sem("s_mhi"), sem("s_msplit")
        s_mT, s_mev = sem("s_mT"), sem("s_mev")
        d_mrow = [sem("d_mrow0"), sem("d_mrow1")]
        s_st, s_exp, s_pv, s_po = sem("s_st"), sem("s_exp"), sem("s_pv"), sem("s_po")
        s_pt, s_rs, s_ctx = sem("s_pt"), sem("s_rs"), sem("s_ctx")
        s_cT, s_cTh, s_cTl = sem("s_cT"), sem("s_cTh"), sem("s_cTl")
        s_last_po, s_last_pt, s_last_rs = sem("s_last_po"), sem("s_last_pt"), sem("s_last_rs")
        s_last_ctx, s_last_cT = sem("s_last_ctx"), sem("s_last_cT")
        s_last_high, s_last_low = sem("s_last_high"), sem("s_last_low")
        s_op, s_acc, d_out = sem("s_op"), sem("s_acc"), sem("d_out")

        def piece(k, wi_t, wo_t):
            half = k % 2
            if k < 2:
                return wi_t[:, :, half * HALF * P:(half + 1) * HALF * P]
            return wo_t[:, half * HALF:(half + 1) * HALF, :]

        x_tiles = x_in.rearrange("b (t p) d -> b p t d", p=P)
        out_tiles = out.rearrange("b (t p) d -> b p t d", p=P)
        wi_flat = wi_in.rearrange("e (k p) f -> p (e k) f", p=P)
        wout_flat = wout_in.rearrange("e (t p) d -> p (e t) d", p=P)
        N_QK = B * QK_TILES

        LAST_OUT, LAST_CONTEXT, LAST_PROJECTED = (7, 0), (1, 2), (3, 4)

        def score_bank(p, j):
            return 4 + j % 2 if before(p, PAIRS - 1) or j < 2 else j - 2

        def row_bank(e):
            return ROW_BANKS[1] if after(e, 0) else ROW_BANKS[0]

        def stack_at(pair, is_k):
            p4 = pair % 4
            return p4 * 2 * HG * S + (p4 // 2) * STACK + (STACK if is_k else 0)

        def wait_used(eng, k, e):
            if k < 2:
                eng.wait_ge(s_h, FT * e + HALF * (k + 1))
            else:
                eng.wait_ge(s_yhalf if k == 2 else s_y, e + 1)

        LOADS_W, LOADS_SMALL = 4, 1
        STACK_LOADS = 2 * NTERM + 1
        block = ctx.enter_context(nc.Block())

        @block.sync
        def _(sp):
            for b in range(B):
                if b == 2:
                    sp.wait_ge(d_w, 16 * LOADS_W)
                sp.dma_start(acc[:, b * TB:(b + 1) * TB, :], x_tiles[b]).then_inc(d_x[b], 16)

            def load_piece(k, e):
                if after(e, 0):
                    sp.wait_ge(w_lo[k], e)
                if k < 2:
                    src = wi_flat[:, bass.ds(e * KT, KT), (k % 2) * HALF * P:(k % 2 + 1) * HALF * P]
                else:
                    src = wout_flat[:, bass.ds(e * FT + (k % 2) * HALF, HALF), :]
                sp.dma_start(piece(k, raw_wi, raw_wo), src).then_inc(d_raw[k], 16)

            def load_rows(e):
                if after(e, 0):
                    sp.wait_ge(s_xdT, e)
                sp.dma_start(xd[:, 0:2, :], xd_d[bass.ds(e * CAP, 2 * P), :].rearrange("(t p) d -> p t d", p=P)
                             ).then_inc(d_xd, 16)
                sp.dma_start(xd[0:CAP - 2 * P, 2, :], xd_d[bass.ds(e * CAP + 2 * P, CAP - 2 * P), :]).then_inc(d_xd, 16)

            def store_rows(e):
                sp.wait_ge(s_yr, 2 * e + 2)
                sp.dma_start(yd_d[bass.ds(e * CAP, 2 * P), :].rearrange("(t p) d -> p t d", p=P), y_rows[:, 0:2, :]
                             ).then_inc(d_y, 16)
                sp.dma_start(yd_d[bass.ds(e * CAP + 2 * P, CAP - 2 * P), :], y_rows[0:CAP - 2 * P, 2, :]).then_inc(d_y, 16)

            def load_stack(b):
                for which, terms in enumerate((Q_TERMS, K_TERMS)):
                    for r, part in enumerate(terms):
                        at = (b % 2) * 2 * STACK + which * STACK
                        dst = stack[r * HD:(r + 1) * HD, at:at + STACK].rearrange("p (h s) -> p h s", s=S)
                        src = parts_d[b, which, part].rearrange("(h d) s -> d h s", d=HD)
                        sp.dma_start(dst, src).then_inc(d_stack, 16)
                at = (b % 2) * 2 * STACK + STACK
                sp.dma_start(stack[MAX_ROW:ROWS, at:at + STACK].rearrange("r (n c) -> r n c", c=P),
                             onesb[0:2, :].unsqueeze(1).to_broadcast([2, STACK // P, P])).then_inc(d_stack, 16)

            sp.wait_ge(d_x[B - 1], 16)
            for k in range(4):
                load_piece(k, 0)
            for k in range(3):
                load_piece(k, 1)
            for n in range(N_QK):
                if n == ROWS_AT:
                    sp.wait_ge(d_scatter, 16 * NT)
                    load_rows(0)
                if n == N_QK - 1:
                    load_rows(1)
                b, m = divmod(n, QK_TILES)
                sp.wait_ge(s_lo, n + 1)
                dst = parts_d[b, m // KT].rearrange("c (m p) s -> p c m s", p=P)[:, :, m % KT, :]
                sp.dma_start(dst, parts[:, n % RING, :, :]).then_inc(d_parts[n % RING], 16)
            load_piece(3, 1)
            for n in range(RING):
                sp.wait_ge(d_parts[n], 16 * ((N_QK - n + RING - 1) // RING))
            load_stack(0)

            def expert(e):
                if before(e, E - 2):
                    load_rows(e + 2)
                if after(e, 0):
                    store_rows(e - 1)
                if after(e, 0) and before(e, E - 1):
                    load_piece(2, e + 1)
                    load_piece(3, e + 1)
                if before(e, E - 2):
                    load_piece(0, e + 2)
                    load_piece(1, e + 2)

            expert(0)
            with sp.Fori(1, E - 2) as e:
                expert(e)
            expert(E - 2)

            expert(E - 1)

            def load_max(g, hg):
                sp.wait_ge(s_mev, g + 1)
                at = (g // GPB % 2) * 2 * STACK + hg * HG * S
                for r in range(2):
                    dst = stack[MAX_ROW + r:MAX_ROW + r + 1, at:at + HG * S].rearrange("r (c t) -> r c t", t=P)
                    sp.dma_start(dst, mrow[16 * r:16 * r + 16, g % 2, :]).then_inc(d_mrow[g % 2], 16)

            load_max(0, 0)
            store_rows(E - 1)
            for b in range(B):
                for hg in range(GPB):
                    g = GPB * b + hg + 1
                    if g < GROUPS:
                        load_max(g, g % GPB)
                    if g == 1:
                        wait_used(sp, 3, E - 1)
                        sp.wait_ge(d_stack, 16 * STACK_LOADS)
                        load_stack(1)
                    if hg == 3 and b + 2 < B:
                        sp.wait_ge(s_exp, 16 * GPB * (b + 1) + 2)
                        sp.wait_ge(d_stack, 16 * STACK_LOADS * (b + 2))
                        load_stack(b + 2)
                    if hg == 2 and b > 0:
                        sp.wait_ge(s_acc, GPB * b + 2)
                        sp.dma_start(out_tiles[b - 1], acc[:, (b - 1) * TB:b * TB, :]).then_inc(d_out, 16)
            for half in range(2):
                t = slice(2 * half, 2 * half + 2)
                sp.wait_ge(s_acc, GPB * B + 1 + half)
                sp.dma_start(out_tiles[B - 1][:, t, :], acc[:, (B - 1) * TB:, :][:, t, :]).then_inc(d_out, 16)
            sp.wait_ge(d_out, 16 * (B + 1))

        @block.gpsimd
        def _(pool):
            pool.memset(ident[:], 0.0).then_inc(s_pool, 1)
            pool.memset(identb[:], 0.0).then_inc(s_pool, 1)
            pool.memset(earlier[:], 1.0).then_inc(s_pool, 1)
            pool.wait_ge(s_pool, 3)
            for m in (ident, identb):
                pool.affine_select(out=m[:], in_=m[:], compare_op=ALU.not_equal, fill=1.0, base=0,
                                   pattern=[[-1, P]], channel_multiplier=1).then_inc(s_const, 1)
            pool.affine_select(out=earlier[:], in_=earlier[:], compare_op=ALU.is_gt, fill=0.0, base=0,
                               pattern=[[1, P]], channel_multiplier=-1).then_inc(s_const, 1)
            pool.memset(onesb[:], 1.0).then_inc(s_const, 1)
            pool.memset(warm[:], 0.0).then_inc(s_warm, 1)
            pool.memset(zeros[:], 0.0).then_inc(s_pool, 1)
            for e in range(E):
                pool.memset(descend[:, e:e + 1], float(E - e)).then_inc(s_const, 1)
                pool.memset(starts[:, e:e + 1], float(e * CAP)).then_inc(s_const, 1)
            pool.iota(m_i[:], [[1, NT * E]], base=0, channel_multiplier=-1).then_inc(s_const, 1)
            pool.iota(dump_i[:], [[P, NT]], base=SLOTS, channel_multiplier=1).then_inc(s_const, 1)
            pool.wait_ge(s_pool, 4)
            pool.wait_ge(d_x[B - 1], 16)
            per = SLOTS // P
            pool.dma_start(xd_d[0:SLOTS, :].rearrange("(p r) d -> p r d", r=per),
                           zeros[:, :].unsqueeze(1).to_broadcast([P, per, D])).then_inc(d_zero, 16)
            pool.wait_ge(s_wTh, 5)
            pool.memset(bvb[:], 1.0).then_inc(s_pool, 1)
            pool.wait_ge(s_pool, 5)
            for kt in range(KT):
                pool.tensor_scalar(bvb[:, kt, :], bvb[:, kt, :], b_cols[:, QK_TILES + kt:QK_TILES + kt + 1], None, ALU.mult).then_inc(s_bvb, 1)
            pool.wait_ge(s_bvb, KT)
            pool.tensor_copy(bvb_h[:], bvb[:]).then_inc(s_bvb, 1)
            pool.wait_ge(s_bvb, KT + 1)
            pool.tensor_tensor(bvb_l[:], bvb[:], bvb_h[:].bitcast(F32), ALU.subtract).then_inc(s_bvb, 1)

            def split_low(k, e):
                pool.wait_ge(w_hi[k], e + 1)
                pool.tensor_tensor(piece(k, wi_l, wo_l), piece(k, raw_wi, raw_wo), piece(k, wi_h, wo_h).bitcast(F32),
                                   ALU.subtract).then_inc(w_lo[k], 1)

            for k in range(3):
                split_low(k, 0)

            pool.wait_ge(d_zero, 16)
            for t in range(NT):
                if t == 0:
                    pool.wait_ge(s_index, 1)
                elif t == ROUTE_TILES[0]:
                    pool.wait_ge(s_index, 2)
                pool.indirect_dma_start(out=xd_d, out_offset=bass.IndirectOffsetOnAxis(ap=to_slot[:, t:t + 1], axis=0),
                                        in_=xn[:, t, :], in_offset=None).then_inc(d_scatter, 16)

            split_low(3, 0)

            def expert(e):
                if after(e, 0):
                    split_low(3, e)
                if before(e, E - 1):
                    split_low(2, e + 1)

            def add_bias(b):
                tiles = slice(b * TB, (b + 1) * TB)
                pool.tensor_tensor(acc[:, tiles, :], acc[:, tiles, :], bias[:, :].unsqueeze(1).to_broadcast([P, TB, D]),
                                   ALU.add).then_inc(s_xb, 1)

            def copy_v(pair, u):
                g = 2 * pair + u
                if after(g, 1):
                    pool.wait_ge(s_pv, TB * g - TB)
                src = vg[:, bass.ds(pair // 2 * TB, TB), bass.ds(pair % 2 * 2 * HG * HD + u * HG * HD, HG * HD)]
                pool.tensor_copy(vslot[:, u, :, :, 0:HD], src.rearrange("p t (j c) -> p t j c", j=HG)
                                 ).then_inc(s_vslot, 1)

            expert(0)
            pool.wait_ge(s_qk, N_QK)
            pool.memset(vslot[:], 0.0).then_inc(s_vz, 1)
            pool.wait_ge(s_bias, 1)
            add_bias(0)
            add_bias(1)
            with pool.Fori(1, E - 1) as e:
                expert(e)
            pool.memset(vslot[:, :, :, :, HD:HD + 1], 1.0).then_inc(s_vz, 1)
            add_bias(2)
            expert(E - 1)
            pool.wait_ge(s_vz, 2)
            copy_v(0, 0)
            copy_v(0, 1)
            add_bias(3)

            pool.wait_ge(s_index, 4)
            pool.wait_ge(d_y, 32 * E)

            def gather(b):
                for t in range(b * TB, (b + 1) * TB):
                    pool.indirect_dma_start(out=y_tok[:, t, :], out_offset=None, in_=yd_d,
                                            in_offset=bass.IndirectOffsetOnAxis(ap=from_slot[:, t:t + 1], axis=0)
                                            ).then_inc(d_gather[b], 16)

            pool.wait_ge(s_xb, B)
            gather(0)
            for b in range(B):
                if b + 1 < B:
                    gather(b + 1)
                tiles = slice(b * TB, (b + 1) * TB)
                pool.wait_ge(d_gather[b], 16 * TB)
                pool.tensor_tensor(y_tok[:, tiles, :], y_tok[:, tiles, :],
                                   weight[:, tiles].unsqueeze(2).to_broadcast([P, TB, D]), ALU.mult).then_inc(s_wy, 1)
                pool.wait_ge(s_wy, b + 1)
                pool.tensor_tensor(acc[:, tiles, :], acc[:, tiles, :], y_tok[:, tiles, :], ALU.add).then_inc(s_comb, 1)
                if b == 0:
                    copy_v(1, 0)
                    copy_v(1, 1)
            with pool.Fori(2, PAIRS) as p:
                copy_v(p, 0)
                copy_v(p, 1)

        @block.scalar
        def _(act):
            act.dma_start(w_rows[:], wqkv_in.rearrange("(m p) d -> p m d", p=P)).then_inc(d_w, 16)
            act.dma_start(wo_rows[:], wo_in.rearrange("(m p) d -> p m d", p=P)).then_inc(d_w, 16)
            act.dma_start(gate_rows[:], gate_in).then_inc(d_w, 16)
            act.dma_start(b_rows[:], bqkv_in.rearrange("(m p) -> m p", p=P)).then_inc(d_w, 16)
            act.dma_start(bias[:], bo_in.rearrange("(a d) -> a d", a=1).to_broadcast([P, D])).then_inc(d_small, 16)

            def weight_banks():
                for kt in range(KT):
                    yield wT_h[:, kt, 512:512 + VG], ps[:, 4 + kt, 0:VG]
                for kt in range(KT):
                    yield wT_h[:, kt, 0:512], ps[:, 2 + kt, :]
                yield b_cols[:], ps[:, 7, 0:3 * KT]

            def root(b):
                act.wait_ge(s_var, b + 1)
                act.activation(vare[:, b, :], vare[:, b, :], ACT.Sqrt).then_inc(s_root, 1)

            act.wait_ge(s_warm, 1)
            def tokens_high(b):
                act.wait_ge(s_xT, b + 1)
                act.activation(xT_h[:, b, :, :], ps[:, XT_BANKS[b % 2]:XT_BANKS[b % 2] + 2, :], ACT.Copy).then_inc(s_xTh, 1)

            act.activation(warm[:], warm[:], ACT.Sqrt)
            root(0)
            for n, (dst, src) in enumerate(weight_banks()):
                act.wait_ge(s_wT, n + 1)
                act.activation(dst, src, ACT.Copy).then_inc(s_wTh, 1)
                if n == KT - 1:
                    root(1)
                    tokens_high(0)

            def split_high(k, e):
                act.wait_ge(d_raw[k], 16 * e + 16)
                if after(e, 0):
                    wait_used(act, k, e - 1)
                act.activation(piece(k, wi_h, wo_h), piece(k, raw_wi, raw_wo), ACT.Copy).then_inc(w_hi[k], 1)

            tokens_high(1)
            root(2)
            for t in range(NT):
                act.wait_ge(s_v, t + 1)
                act.activation(vg[:, t, :], ps[:, 6 + t % 2, 0:VG], ACT.Copy).then_inc(s_vg, 1)
                if t == TB - 1:
                    act.wait_ge(s_wT, 6)
                    act.activation(woT_h[:], ps[:, 2, :].rearrange("p (k d) -> p k d", k=KT), ACT.Copy).then_inc(s_wTh, 1)
                if t == TB + 1:
                    root(3)
                if t in (TB + 1, 2 * TB - 1):
                    tokens_high(2 if t == TB + 1 else 3)
                if t in (TB - 1, TB, 2 * TB - 1, 3 * TB - 1):
                    split_high((TB - 1, TB, 2 * TB - 1, 3 * TB - 1).index(t), 0)
            act.activation(warm[:], warm[:], ACT.Gelu)
            act.wait_ge(s_wTh, 6)

            def rows_high(e):
                act.wait_ge(s_xdT, e + 1)
                if after(e, 0):
                    wait_used(act, 1, e - 1)
                act.activation(xdT_h[:], ps[:, row_bank(e):row_bank(e) + 2, 0:CAP], ACT.Copy).then_inc(s_xdh, 1)

            def middle_part(n):
                act.wait_ge(s_r, n + 1)
                act.activation(parts[:, n % RING, 1, :], qkr[:, n % QKR, :], ACT.Copy).then_inc(s_mid, 1)

            for n in range(N_QK):
                act.wait_ge(s_qk, n + 1)
                if n >= RING:
                    act.wait_ge(d_parts[n % RING], 16 * (n // RING))
                act.activation(parts[:, n % RING, 0, :], ps[:, QK_BANKS[n % 3], :], ACT.Identity,
                               bias=b_cols[:, n % QK_TILES:n % QK_TILES + 1]).then_inc(s_hi, 1)
                if n == N_QK - 1:
                    rows_high(0)
                if n:
                    middle_part(n - 1)
            middle_part(N_QK - 1)

            def turn_max(g, u):
                act.wait_ge(s_mT, g + 1)
                act.activation(mrow[:, u, :], ps[0:32, 7, 0:P // 2].bitcast(BF16), ACT.Copy).then_inc(s_mev, 1)

            def gelu(e, i):
                n = FT * e + i
                act.wait_ge(s_h, n + 1)
                if after(n, 1):
                    act.wait_ge(s_gl, n - 1)
                act.activation(g32[:, i % 2, :], ps[:, i % 2, 0:CAP], ACT.Gelu).then_inc(s_gelu, 1)

            def expert(e):
                for i in range(FT):
                    gelu(e, i)
                    if i == 1 and after(e, 0):
                        split_high(3, e)
                    if i == 5 and before(e, E - 1):
                        split_high(0, e + 1)
                if before(e, E - 1):
                    rows_high(e + 1)
                    split_high(1, e + 1)
                    split_high(2, e + 1)
                else:
                    turn_max(0, 0)
                    act.wait_ge(s_index, 2)
                    act.activation(t_b[:], t_a[:], ACT.Exp).then_inc(s_exp8, 1)
                act.wait_ge(s_y, e + 1)
                if after(e, 0):
                    act.wait_ge(s_yb, e)
                act.activation(yT[:], ps[:, 2:4, 0:CAP], ACT.Copy).then_inc(s_yT, 1)

            expert(0)
            with act.Fori(1, E - 1) as e:
                expert(e)
            expert(E - 1)

            def take_out(g, u):
                act.wait_ge(s_pv, TB * g + TB)
                if after(g, 1):
                    act.wait_ge(s_pt, g - 1)
                act.activation(poT[:, u, :], ps[:, 6, :], ACT.Copy).then_inc(s_po, 1)

            def context_high(q):
                act.wait_ge(s_cT, q + 1)
                act.activation(ctxT_h[:], ps[:, 7, :], ACT.Copy).then_inc(s_cTh, 1)

            def group(p, u):
                g = 2 * p + u
                for st in range(TB):
                    if after(g, 0):
                        act.wait_ge(s_pv, TB * g + st + 1 - TB)
                    for j in range(HG):
                        n = 16 * g + HG * st + j
                        act.wait_ge(s_st, n + 1)
                        act.activation(probs[:, st, j, :], ps[:, score_bank(p, j), :], ACT.Exp, scale=SCALE
                                       ).then_inc(s_exp, 1)
                    if st == 0 and after(g, 0):
                        take_out(g - 1, 1 - u)
                    if st == 1 and (u == 0 or before(p, PAIRS - 1)):
                        turn_max(g + 1, 1 - u)
                if u == 0 and after(p, 0):
                    context_high(p - 1)

            act.sem_inc(s_exp, 2)
            act.wait_ge(s_gl, FT * E)
            wait_used(act, 3, E - 1)
            group(0, 0)
            group(0, 1)
            with act.Fori(1, PAIRS - 1) as p:
                group(p, 0)
                group(p, 1)
            group(PAIRS - 1, 0)
            group(PAIRS - 1, 1)
            halves = [slice(0, S // 2), slice(S // 2, S)]
            act.wait_ge(s_pv, TB * GROUPS)
            for half, col in enumerate(halves):
                act.activation(poT[:, 1, col], ps[:, 6, col], ACT.Copy).then_inc(s_last_po, 1)
            for half, col in enumerate(halves):
                act.wait_ge(s_last_cT, half + 1)
                act.activation(ctxT_h[:, col], ps[:, LAST_CONTEXT[half], col], ACT.Copy).then_inc(s_last_high, 1)

        @block.vector
        def _(dve):
            ln, route = [0], [0]

            def chain(counter, semaphore, instruction):
                instruction.then_inc(semaphore, 1)
                counter[0] += 1
                dve.wait_ge(semaphore, counter[0])

            def statistics(b):
                dve.wait_ge(d_x[b], 16)
                for t in range(TB):
                    last = dve.bn_stats(stats[:, t, :], acc[:, b * TB + t, :])
                chain(ln, s_ln, last)
                for t in range(TB):
                    last = dve.bn_aggr(mv[:, b, t, :], stats[:, t, :])
                chain(ln, s_ln, last)
                dve.tensor_scalar(vare[:, b, :], mv[:, b, :, 1], EPS, None, ALU.add).then_inc(s_var, 1)

            def normalise_tokens(b):
                dve.wait_ge(s_root, b + 1)
                chain(ln, s_ln, dve.reciprocal(rstd[:, b, :], vare[:, b, :]))
                for t in range(TB):
                    last = dve.tensor_scalar(xn[:, b * TB + t, :], acc[:, b * TB + t, :], mv[:, b, t, 0:1],
                                             rstd[:, b, t:t + 1], ALU.subtract, ALU.mult)
                last.then_inc(s_xn, 1)

            def weight_banks():
                for kt in range(KT):
                    yield wT_l[:, kt, 512:512 + VG], ps[:, 4 + kt, 0:VG], wT_h[:, kt, 512:512 + VG]
                for kt in range(KT):
                    yield wT_l[:, kt, 0:512], ps[:, 2 + kt, :], wT_h[:, kt, 0:512]

            dve.wait_ge(s_const, 4 + 2 * E + 2)
            dve.tensor_scalar(m_low[:], m_i[:], E - 1, None, ALU.bitwise_and).then_inc(s_mask, 1)
            dve.tensor_scalar(m_later[:], m_i[:], 0.0, None, ALU.is_gt).then_inc(s_mask, 1)
            dve.wait_ge(s_mask, 2)
            dve.tensor_scalar(m_same[:], m_low[:], 0.0, None, ALU.is_equal).then_inc(s_mask, 1)
            dve.tensor_copy(dump[:], dump_i[:]).then_inc(s_mask, 1)
            dve.wait_ge(s_mask, 4)
            dve.tensor_tensor(tiles_before[:], m_same[:], m_later[:], ALU.mult).then_inc(s_mask, 1)
            statistics(0)
            normalise_tokens(0)
            statistics(1)
            banks = list(weight_banks())

            def weights_low(n):
                dst, src, high = banks[n]
                dve.wait_ge(s_wTh, n + 1)
                dve.tensor_tensor(dst, src, high.bitcast(F32), ALU.subtract).then_inc(s_wTl, 1)

            weights_low(0)
            weights_low(1)
            normalise_tokens(1)

            def tokens_low(b):
                dve.wait_ge(s_xTh, b + 1)
                dve.tensor_tensor(xT_l[:, b, :, :], ps[:, XT_BANKS[b % 2]:XT_BANKS[b % 2] + 2, :],
                                  xT_h[:, b, :, :].bitcast(F32), ALU.subtract).then_inc(s_xTl, 1)

            def per_tile(column, n):
                return column[:, 0:n].unsqueeze(2).to_broadcast([P, n, E])

            def per_expert(row, n):
                return row[:, :].unsqueeze(1).to_broadcast([P, n, E])

            def choose_experts(r):
                n = ROUTE_TILES[r]
                a, c, hot = t_a[:, 0:n, :], t_c[:, 0:n, :], onehb[:, 0:n, :]
                dve.wait_ge(s_vg, n)
                logits = vg[:, 0:n, D:D + E]
                chain(route, s_route, dve.tensor_reduce(c_a[:, 0:n], logits, AX_X, ALU.max))
                chain(route, s_route, dve.tensor_tensor(a, logits, per_tile(c_a, n), ALU.subtract))
                chain(route, s_route, dve.scalar_tensor_tensor(out=c, in0=a, scalar=0.0, in1=per_expert(descend, n),
                                                               op0=ALU.is_equal, op1=ALU.mult))
                chain(route, s_route, dve.tensor_reduce(c_b[:, 0:n], c, AX_X, ALU.max))
                dve.tensor_tensor(hot, c, per_tile(c_b, n), ALU.is_equal).then_inc(s_oneh, 1)

            def tile_counts(r):
                n = ROUTE_TILES[r]
                c = t_c[:, 0:n, :]
                dve.wait_ge(s_count, r + 1)
                dve.tensor_copy(countsb[0:n * E, :], ps[0:n * E, ROUTE_BANK, 256:256 + P]).then_inc(s_countb, 1)
                chain(route, s_route, dve.tensor_tensor(c, onehb[:, 0:n, :], per_expert(starts, n), ALU.mult))
                chain(route, s_route, dve.tensor_reduce(c_c[:, 0:n], c, AX_X, ALU.add))

            def slots(r):
                n = ROUTE_TILES[r]
                c, a, b, d = t_c[:, 0:n, :], c_c[:, 0:n], c_b[:, 0:n], c_d[:, 0:n]
                sent = ROUTE_TILES[r - 1] if r else 0
                dve.wait_ge(s_rank, r + 1)
                ranks = ps[:, ROUTE_BANK, 0:n * E].rearrange("p (t e) -> p t e", e=E)
                chain(route, s_route, dve.tensor_tensor(c, ranks, onehb[:, 0:n, :], ALU.mult))
                chain(route, s_route, dve.tensor_reduce(b, c, AX_X, ALU.add))
                chain(route, s_route, dve.tensor_tensor(a, a, b, ALU.add))
                chain(route, s_route, dve.tensor_tensor(d, a, dump[:, 0:n], ALU.subtract))
                chain(route, s_route, dve.scalar_tensor_tensor(out=d, in0=b, scalar=float(CAP), in1=d,
                                                               op0=ALU.is_lt, op1=ALU.mult))
                dve.tensor_tensor(to_slot[:, sent:n], c_d[:, sent:n], dump[:, sent:n], ALU.add).then_inc(s_index, 1)

            tokens_low(0)
            statistics(2)
            tokens_low(1)
            weights_low(2)
            weights_low(3)
            normalise_tokens(2)
            statistics(3)
            normalise_tokens(3)
            tokens_low(2)
            tokens_low(3)
            dve.wait_ge(s_wTh, 6)
            dve.tensor_tensor(woT_l[:], ps[:, 2, :].rearrange("p (k d) -> p k d", k=KT), woT_h[:].bitcast(F32),
                              ALU.subtract).then_inc(s_wTl, 1)
            choose_experts(0)
            tile_counts(0)
            slots(0)
            choose_experts(1)
            tile_counts(1)
            slots(1)
            def split_low(k, e):
                dve.wait_ge(w_hi[k], e + 1)
                dve.tensor_tensor(piece(k, wi_l, wo_l), piece(k, raw_wi, raw_wo), piece(k, wi_h, wo_h).bitcast(F32),
                                  ALU.subtract).then_inc(w_lo[k], 1)

            def low_part(n):
                dve.wait_ge(s_mid, n + 1)
                dve.tensor_tensor(parts[:, n % RING, 2, :], qkr[:, n % QKR, :], parts[:, n % RING, 1, :], ALU.subtract
                                  ).then_inc(s_lo, 1)

            def rows_low(e):
                dve.wait_ge(s_xdh, e + 1)
                dve.tensor_tensor(xdT_l[:], ps[:, row_bank(e):row_bank(e) + 2, 0:CAP], xdT_h[:].bitcast(F32), ALU.subtract
                                  ).then_inc(s_xdl, 1)

            for n in range(N_QK):
                if n == N_QK - 1:
                    rows_low(0)
                dve.wait_ge(s_hi, n + 1)
                if n >= QKR:
                    dve.wait_ge(s_lo, n - QKR + 1)
                dve.scalar_tensor_tensor(out=qkr[:, n % QKR, :], in0=ps[:, QK_BANKS[n % 3], :],
                                         scalar=b_cols[:, n % QK_TILES:n % QK_TILES + 1],
                                         in1=parts[:, n % RING, 0, :], op0=ALU.add, op1=ALU.subtract).then_inc(s_r, 1)
                if n:
                    low_part(n - 1)
            low_part(N_QK - 1)
            dve.wait_ge(s_bvp, 1)
            dve.wait_ge(d_small, 16 * LOADS_SMALL)
            dve.tensor_tensor(bias[:], ps[:, 7, 0:D], bias[:], ALU.add).then_inc(s_bias, 1)

            def reduce_max(g, u, c):
                dve.wait_ge(s_smax, 8 * g + c + 1)
                col = c // 2 * TB + c % 2 * 2
                dve.tensor_reduce(negm[:, u, col:col + 2], ps[:, 2 * (c % 2):2 * (c % 2) + 2, :], AX_X, ALU.max,
                                  negate=True).then_inc(s_red, 1)

            def split_max(g, u):
                dve.wait_ge(s_red, 8 * g + 8)
                if after(g, 1):
                    dve.wait_ge(s_mT, g - 1)
                dve.tensor_copy(mpart[:, u, 0, :], negm[:, u, :]).then_inc(s_mhi, 1)
                dve.wait_ge(s_mhi, g + 1)
                dve.tensor_tensor(mpart[:, u, 1, :], negm[:, u, :], mpart[:, u, 0, :], ALU.subtract
                                  ).then_inc(s_msplit, 1)

            def first_max(e, half):
                dve.wait_ge(s_smax, 2 * e + half + 1)
                dve.tensor_reduce(negm[:].rearrange("p u c -> p (u c)")[:, bass.ds(e * TB + 2 * half, 2)], ps[:, 4:6, :], AX_X, ALU.max, negate=True
                                  ).then_inc(s_red, 1)

            def weights_of_tokens():
                chain(route, s_route, dve.tensor_scalar(keep[:], c_b[:], float(CAP), None, ALU.is_lt))
                dve.tensor_tensor(from_slot[:], c_c[:], keep[:], ALU.mult).then_inc(s_index, 1)
                dve.wait_ge(s_exp8, 1)
                chain(route, s_route, dve.tensor_reduce(c_a[:], t_b[:], AX_X, ALU.add))
                chain(route, s_route, dve.reciprocal(weight[:], c_a[:]))
                dve.tensor_tensor(weight[:], weight[:], keep[:], ALU.mult).then_inc(s_index, 1)

            def rows_back(e):
                dve.wait_ge(s_yb, e + 1)
                if after(e, 0):
                    dve.wait_ge(d_y, 32 * e)
                dve.tensor_copy(y_rows[:, 0:2, :], ps[:, 6, :].rearrange("p (t d) -> p t d", d=D)).then_inc(s_yr, 1)
                dve.tensor_copy(y_rows[0:CAP - 2 * P, 2, :], ps[0:CAP - 2 * P, 7, 0:D]).then_inc(s_yr, 1)

            def expert(e, max_heads):
                for i in range(FT):
                    n = FT * e + i
                    dve.wait_ge(s_gelu, n + 1)
                    if i % HALF == 0 and after(e, 0):
                        wait_used(dve, 2 + i // HALF, e - 1)
                    dve.tensor_copy(gh[:, i, :], g32[:, i % 2, :]).then_inc(s_gh, 1)
                    dve.wait_ge(s_gh, n + 1)
                    dve.tensor_tensor(gl[:, i, :], g32[:, i % 2, :], gh[:, i, :].bitcast(F32), ALU.subtract
                                      ).then_inc(s_gl, 1)
                    if i == 3 and after(e, 0):
                        rows_back(e - 1)
                    if i == 6 and before(e, E - 1):
                        split_low(0, e + 1)
                if before(e, E - 1):
                    rows_low(e + 1)
                    split_low(1, e + 1)
                for head in max_heads:
                    first_max(head, 0)
                    first_max(head, 1)

            dve.wait_ge(s_lo, N_QK)
            for n in range(RING - 3):
                dve.wait_ge(d_parts[n], 16 * (N_QK // RING))
            expert(0, [])
            expert(1, [0, 1])
            with dve.Fori(2, E - 1) as e:
                expert(e, [e])
            split_max(0, 0)
            expert(E - 1, [E - 1])
            weights_of_tokens()

            dve.sem_inc(s_acc, 2)

            def normalise(g, u):
                dve.wait_ge(s_pt, g + 1)
                rows = ps[:, 7, :].rearrange("p (i j c) -> p i j c", i=TB, j=HG)
                dve.reciprocal(rsum[:, u], rows[:, :, :, HD]).then_inc(s_rs, 1)
                dve.wait_ge(s_rs, g + 1)
                dst = ctx_sb[:, :, u * HG * HD:(u + 1) * HG * HD].rearrange("p i (j c) -> p i j c", j=HG)
                dve.tensor_tensor(dst, rows[:, :, :, 0:HD], rsum[:, u].unsqueeze(3).to_broadcast([P, TB, HG, HD]),
                                  ALU.mult).then_inc(s_ctx, 1)

            def context_low(q):
                dve.wait_ge(s_cTh, q + 1)
                dve.tensor_tensor(ctxT_l[:], ps[:, 7, :], ctxT_h[:].bitcast(F32), ALU.subtract).then_inc(s_cTl, 1)

            def accumulate(q, half, bank=7):
                dve.wait_ge(s_op, 2 * q + half + 1)
                dve.wait_ge(s_comb, q // 2 + 1)
                tiles = acc[:, bass.ds(q // 2 * TB + 2 * half, 2), :]
                dve.tensor_tensor(tiles, ps[:, bank, :].rearrange("p (i d) -> p i d", i=2), tiles, ALU.add
                                  ).then_inc(s_acc, 1)

            def group(p, u):
                g = 2 * p + u
                more = before(p, PAIRS - 1)
                for st in range(TB):
                    if more:
                        reduce_max(g + 2, u, 2 * st)
                    if st == 0 and not after(g, 0):
                        rows_back(E - 1)
                    if more:
                        reduce_max(g + 2, u, 2 * st + 1)
                    if st == 0 and u == 1 and after(p, 0):
                        accumulate(p - 1, 0)
                    if st == 2 and after(g, 0):
                        normalise(g - 1, 1 - u)
                if more:
                    split_max(g + 2, u)
                if u == 0 and after(p, 0):
                    context_low(p - 1)
                if u == 1 and after(p, 0):
                    accumulate(p - 1, 1)

            split_max(1, 1)
            group(0, 0)
            group(0, 1)
            with dve.Fori(1, PAIRS - 1) as p:
                group(p, 0)
                group(p, 1)
            group(PAIRS - 1, 0)
            group(PAIRS - 1, 1)
            for half in range(2):
                t = slice(2 * half, 2 * half + 2)
                dve.wait_ge(s_last_pt, half + 1)
                rows = ps[:, LAST_OUT[half], half * S // 2:(half + 1) * S // 2].rearrange("p (i j c) -> p i j c", i=2, j=HG)
                dve.reciprocal(rsum[:, 1, t], rows[:, :, :, HD]).then_inc(s_last_rs, 1)
                dve.wait_ge(s_last_rs, half + 1)
                dst = ctx_sb[:, t, HG * HD:].rearrange("p i (j c) -> p i j c", j=HG)
                dve.tensor_tensor(dst, rows[:, :, :, 0:HD], rsum[:, 1, t].unsqueeze(3).to_broadcast([P, 2, HG, HD]),
                                  ALU.mult).then_inc(s_last_ctx, 1)
            for half in range(2):
                col = slice(half * S // 2, (half + 1) * S // 2)
                dve.wait_ge(s_last_high, half + 1)
                dve.tensor_tensor(ctxT_l[:, col], ps[:, LAST_CONTEXT[half], col], ctxT_h[:, col].bitcast(F32),
                                  ALU.subtract).then_inc(s_last_low, 1)
            for half in range(2):
                accumulate(PAIRS - 1, half, LAST_PROJECTED[half])

        @block.tensor
        def _(pe):
            pe.wait_ge(s_const, 4)

            def keep_warm(products, bank):
                for _ in range(products):
                    pe.matmul(ps[:, bank, 0:P], onesb[:], onesb[:], start=True, stop=True)

            keep_warm(48, 0)

            def turn(dst, src, identity):
                return pe.transpose(dst, src, identity)

            def product(dst, w_parts, x_parts, first, last):
                (wh, wl), (xh, xl) = w_parts, x_parts
                pe.matmul(dst, wh, xh, start=first, stop=False)
                pe.matmul(dst, wl, xh, start=False, stop=False)
                return pe.matmul(dst, wh, xl, start=False, stop=last)

            def turn_tokens(b):
                pe.wait_ge(s_xn, b + 1)
                if b >= 2:
                    pe.wait_ge(s_xTl, b - 1)
                for kt in range(KT):
                    for t in range(TB):
                        last = turn(ps[:, XT_BANKS[b % 2] + kt, t * P:(t + 1) * P], xn[:, b * TB + t, kt * P:(kt + 1) * P], ident[:])
                last.then_inc(s_xT, 1)

            pe.wait_ge(d_w, 16 * LOADS_W)
            for kt in range(KT):
                k = slice(kt * P, (kt + 1) * P)
                for m in range(2):
                    turn(ps[:, 4 + kt, m * P:(m + 1) * P], w_rows[:, 4 + m, k], ident[:])
                turn(ps[:, 4 + kt, 2 * P:2 * P + E], gate_rows[:, k], ident[0:E, 0:E]).then_inc(s_wT, 1)
            turn_tokens(0)
            for kt in range(KT):
                k = slice(kt * P, (kt + 1) * P)
                for m in range(4):
                    last = turn(ps[:, 2 + kt, m * P:(m + 1) * P], w_rows[:, m, k], ident[:])
                last.then_inc(s_wT, 1)
            turn(ps[:, 7, 0:3 * KT], b_rows[:], ident[0:3 * KT, 0:3 * KT]).then_inc(s_wT, 1)

            def turn_output_weights():
                pe.wait_ge(s_wTl, 3)
                for kt in range(KT):
                    for m in range(KT):
                        last = turn(ps[:, 2, kt * D + m * P:kt * D + (m + 1) * P], wo_rows[:, m, kt * P:(kt + 1) * P], ident[:])
                last.then_inc(s_wT, 1)

            keep_warm(24, 6)
            pe.wait_ge(s_wTl, 2)
            turn_tokens(1)
            pe.wait_ge(s_wTh, 5)
            hot = onehb[:].rearrange("p t e -> p (t e)")

            def count(r):
                rows = ROUTE_TILES[r] * E
                pe.wait_ge(s_oneh, r + 1)
                pe.matmul(ps[0:rows, ROUTE_BANK, 256:256 + P], hot[:, 0:rows], onesb[:], start=True, stop=True
                          ).then_inc(s_count, 1)

            def rank(r):
                rows = ROUTE_TILES[r] * E
                pe.wait_ge(s_countb, r + 1)
                pe.wait_ge(s_mask, 5)
                pe.matmul(ps[:, ROUTE_BANK, 0:rows], earlier[:], hot[:, 0:rows], start=True, stop=False)
                pe.matmul(ps[:, ROUTE_BANK, 0:rows], countsb[0:rows, :], tiles_before[0:rows, 0:rows],
                          start=False, stop=True).then_inc(s_rank, 1)

            for b in range(B):
                if b == 3:
                    pe.wait_ge(s_wTl, 4)
                    count(0)
                if b == 2:
                    turn_tokens(3)
                pe.wait_ge(s_xTl, b + 1)
                for i in range(TB):
                    t = b * TB + i
                    if i == 1 and b == 3:
                        rank(0)
                    if i == 2 and b == 1:
                        turn_tokens(2)
                    if t >= 2:
                        pe.wait_ge(s_vg, t - 1)
                    for kt in range(KT):
                        col = slice(i * P, (i + 1) * P)
                        last = product(ps[:, 6 + t % 2, 0:VG], (xT_h[:, b, kt, col], xT_l[:, b, kt, col]),
                                       (wT_h[:, kt, 2 * D:], wT_l[:, kt, 2 * D:]), kt == 0, kt == KT - 1)
                    last.then_inc(s_v, 1)
                if b == 0:
                    turn_output_weights()

            def project_bias():
                pe.wait_ge(s_vg, NT)
                pe.wait_ge(s_wTl, 5)
                pe.wait_ge(s_bvb, KT + 2)
                for kt in range(KT):
                    last = product(ps[:, 7, 0:D], (bvb_h[:, kt, :], bvb_l[:, kt, :]),
                                   (woT_h[:, kt, :], woT_l[:, kt, :]), kt == 0, kt == KT - 1)
                last.then_inc(s_bvp, 1)

            def turn_rows(e):
                pe.wait_ge(d_xd, 32 * e + 32)
                if after(e, 2):
                    pe.wait_ge(s_red, 2 * e - 2)
                elif after(e, 1):
                    pe.wait_ge(s_xdl, 2)
                elif after(e, 0):
                    pe.wait_ge(s_r, N_QK)
                for kt in range(KT):
                    for r, (at, rows) in enumerate(ROW_TILES):
                        last = turn(ps[:, row_bank(e) + kt, at:at + rows], xd[0:rows, r, kt * P:(kt + 1) * P], ident[0:rows, 0:rows])
                last.then_inc(s_xdT, 1)

            for n in range(N_QK):
                b, m = divmod(n, QK_TILES)
                if n == 1:
                    count(1)
                    rank(1)
                if n == 4:
                    project_bias()
                if n == 0:
                    pe.wait_ge(s_xTl, B)
                elif n == 2:
                    pe.wait_ge(s_vg, NT)
                elif n > 2:
                    pe.wait_ge(s_r, n - 2)
                for kt in range(KT):
                    col = slice(m * P, (m + 1) * P)
                    last = product(ps[:, QK_BANKS[n % 3], :], (wT_h[:, kt, col], wT_l[:, kt, col]),
                                   (xT_h[:, b, kt, :], xT_l[:, b, kt, :]), kt == 0, kt == KT - 1)
                last.then_inc(s_qk, 1)
            turn_rows(0)

            def turn_max(g, u):
                pe.wait_ge(s_msplit, g + 1)
                turn(ps[0:2 * HG * TB, 7, 0:P // 2].bitcast(BF16), mpart[:, u].rearrange("p r c -> p (r c)"), identb[:]
                     ).then_inc(s_mT, 1)

            def first_max(e, half, expert):
                if half or not after(expert, 1) and e:
                    pe.wait_ge(s_red, 2 * e + half)
                elif before(expert, E - 1):
                    pe.wait_ge(s_xdl, expert + 2)
                for i in range(2):
                    last = pe.matmul(ps[:, 4 + i, :], stack[0:MAX_ROW, bass.ds(e * S + (2 * half + i) * P, P)],
                                     stack[0:MAX_ROW, bass.ds(e * S + STACK, S)], start=True, stop=True)
                last.then_inc(s_smax, 1)

            def turn_back(e):
                pe.wait_ge(s_yT, e + 1)
                if after(e, 0):
                    pe.wait_ge(s_yr, 2 * e)
                for r, (at, rows) in enumerate(ROW_TILES):
                    for kt in range(KT):
                        to = r % 2 * D + kt * P
                        last = turn(ps[0:rows, 6 + r // 2, to:to + P], yT[:, kt, at:at + rows], ident[:])
                last.then_inc(s_yb, 1)

            def expert(e, max_at):
                for i in range(FT):
                    n = FT * e + i
                    if i % HALF == 0:
                        pe.wait_ge(w_lo[i // HALF], e + 1)
                    if i == 0:
                        pe.wait_ge(s_xdl, e + 1)
                    if after(n, 1):
                        pe.wait_ge(s_gelu, n - 1)
                    for kt in range(KT):
                        col = slice(i * P, (i + 1) * P)
                        last = product(ps[:, i % 2, 0:CAP], (wi_h[:, kt, col], wi_l[:, kt, col]),
                                       (xdT_h[:, kt, :], xdT_l[:, kt, :]), kt == 0, kt == KT - 1)
                    last.then_inc(s_h, 1)
                    if i == 6 and not before(e, E - 1):
                        pe.wait_ge(s_yr, 2 * E - 2)
                        turn_max(0, 0)
                    if i == 2 and after(e, 0):
                        turn_back(e - 1)
                    if i == 5 and before(e, E - 1):
                        turn_rows(e + 1)
                if after(e, 0):
                    pe.wait_ge(s_yT, e)
                for i in range(FT):
                    if i % HALF == 0:
                        pe.wait_ge(w_lo[2 + i // HALF], e + 1)
                    pe.wait_ge(s_gl, FT * e + i + 1)
                    for m in range(KT):
                        col = slice(m * P, (m + 1) * P)
                        last = product(ps[:, 2 + m, 0:CAP], (wo_h[:, i, col], wo_l[:, i, col]),
                                       (gh[:, i, :], gl[:, i, :]), i == 0, i == FT - 1)
                    if i == HALF - 1:
                        last.then_inc(s_yhalf, 1)
                    if i == FT - 1:
                        last.then_inc(s_y, 1)
                    if i in max_at:
                        which = max_at.index(i)
                        if len(max_at) == 4 and which == 0:
                            pe.wait_ge(d_stack, 16 * STACK_LOADS)
                        first_max(which // 2 if len(max_at) == 4 else e, which % 2, e)

            expert(0, ())
            expert(1, (3, 5, 6, 7))
            with pe.Fori(2, E - 1) as e:
                expert(e, (4, 7))
            expert(E - 1, (1, 4))
            pe.wait_ge(s_gelu, FT * E)
            pe.wait_ge(s_red, 2 * E)
            pe.wait_ge(s_mev, 1)
            woT_hf, woT_lf = (m[:].rearrange("p k d -> p (k d)") for m in (woT_h, woT_l))

            def max_scores(p, u, c):
                n = 8 * (2 * p + u) + c
                if after(n, 1):
                    pe.wait_ge(s_red, n - 1)
                at = (u * HG + c // 2) * S
                for i in range(2):
                    col = at + (c % 2 * 2 + i) * P
                    last = pe.matmul(ps[:, 2 * (c % 2) + i, :], stack[0:MAX_ROW, bass.ds(stack_at(p, False) + col, P)],
                                     stack[0:MAX_ROW, bass.ds(stack_at(p, True) + at, S)], start=True, stop=True)
                last.then_inc(s_smax, 1)

            def scores(p, u, st, j):
                n = 16 * (2 * p + u) + HG * st + j
                if before(p, PAIRS - 1) or (u == 0 and st == 0 and j < 2):
                    pe.wait_ge(s_exp, n + 1)
                elif u == 0 and st == 0:
                    pe.wait_ge(s_red, 8 * GROUPS)
                else:
                    pe.wait_ge(s_exp, n - 1)
                at = (u * HG + j) * S
                pe.matmul(ps[:, score_bank(p, j), :], stack[0:ROWS, bass.ds(stack_at(p, True) + at + st * P, P)],
                          stack[0:ROWS, bass.ds(stack_at(p, False) + at, S)], start=True, stop=True).then_inc(s_st, 1)

            def weigh(g, u, st, half):
                if st == 0 and half:
                    return
                pe.wait_ge(s_exp, 16 * g + HG * st + HG + 2)
                if st == 0:
                    pe.wait_ge(s_vslot, g + 1)
                    if after(g, 0):
                        pe.wait_ge(s_po, g)
                    else:
                        pe.wait_ge(s_yr, 2 * E)
                col = slice(half * S // 2, (half + 1) * S // 2) if st else slice(0, S)
                for j in range(HG):
                    last = pe.matmul(ps[32 * j:32 * j + 32, 6, col], vslot[:, u, st, j, :], probs[:, st, j, col],
                                     start=(st == 0), stop=(st == TB - 1 and half == 1))
                if half or st == 0:
                    last.then_inc(s_pv, 1)

            def turn_out(g, u):
                pe.wait_ge(s_po, g + 1)
                for i in range(TB):
                    last = turn(ps[:, 7, i * P:(i + 1) * P], poT[:, u, i * P:(i + 1) * P], ident[:])
                last.then_inc(s_pt, 1)

            def turn_context(q):
                pe.wait_ge(s_ctx, 2 * q + 2)
                for i in range(TB):
                    last = turn(ps[:, 7, i * P:(i + 1) * P], ctx_sb[:, i, :], ident[:])
                last.then_inc(s_cT, 1)

            def project(q, half, bank=7):
                rows = bass.ds(q % 2 * D, D)
                for i in range(2):
                    col = slice((2 * half + i) * P, (2 * half + i + 1) * P)
                    last = product(ps[:, bank, i * D:(i + 1) * D], (ctxT_h[:, col], ctxT_l[:, col]),
                                   (woT_hf[:, rows], woT_lf[:, rows]), True, True)
                last.then_inc(s_op, 1)

            def group(p, u):
                g = 2 * p + u
                more = before(p, PAIRS - 1)
                if more and u == 0:
                    pe.wait_ge(d_stack, 16 * STACK_LOADS * ((p + 1) // 2 + 1))
                pe.wait_ge(d_mrow[u], 32 * p + 32)
                for st in range(TB):
                    for j in range(HG):
                        scores(p, u, st, j)
                        if j % 2 == 0:
                            if more:
                                max_scores(p + 1, u, 2 * st + j // 2)
                        elif st:
                            weigh(g, u, st - 1, j // 2)
                        elif after(g, 0):
                            weigh(g - 1, 1 - u, TB - 1, j // 2)
                        elif j == 1:
                            turn_back(E - 1)
                    if st == 0 and u == 1 and after(p, 0):
                        pe.wait_ge(s_cTh, p)
                        pe.wait_ge(s_cTl, p)
                        project(p - 1, 0)
                    if st == 1 and (u == 0 or more):
                        pe.wait_ge(s_mev, g + 1)
                        if after(g, 1):
                            pe.wait_ge(s_ctx, g - 1)
                        if after(p, 0):
                            pe.wait_ge(s_acc, 2 * p + u)
                        turn_max(g + 1, 1 - u)
                    if st == 2 and after(g, 0):
                        if u == 0 or more:
                            pe.wait_ge(s_mev, g + 2)
                        else:
                            pe.wait_ge(s_acc, 2 * p + 1)
                        turn_out(g - 1, 1 - u)
                    if st == 3 and u == 0 and after(p, 0):
                        turn_context(p - 1)
                    if st == 3 and u == 1 and after(p, 0):
                        pe.wait_ge(s_ctx, g)
                        project(p - 1, 1)

            group(0, 0)
            group(0, 1)
            with pe.Fori(1, PAIRS - 1) as p:
                group(p, 0)
                group(p, 1)
            group(PAIRS - 1, 0)
            group(PAIRS - 1, 1)
            for half in range(2):
                weigh(GROUPS - 1, 1, TB - 1, half)
            for half in range(2):
                pe.wait_ge(s_last_po, half + 1)
                if half == 0:
                    pe.wait_ge(s_acc, 2 * PAIRS)
                    pe.wait_ge(s_exp, 16 * GROUPS + 2)
                for i in (2 * half, 2 * half + 1):
                    last = turn(ps[:, LAST_OUT[half], i * P:(i + 1) * P], poT[:, 1, i * P:(i + 1) * P], ident[:])
                last.then_inc(s_last_pt, 1)
            for half in range(2):
                pe.wait_ge(s_last_ctx, half + 1)
                for i in (2 * half, 2 * half + 1):
                    last = turn(ps[:, LAST_CONTEXT[half], i * P:(i + 1) * P], ctx_sb[:, i, :], ident[:])
                last.then_inc(s_last_cT, 1)
            for half in range(2):
                pe.wait_ge(s_last_high, half + 1)
                pe.wait_ge(s_last_low, half + 1)
                project(PAIRS - 1, half, LAST_PROJECTED[half])


_INS = ["L0_attn_hidden_states", "L0_attn_Wqkv_w", "L0_attn_Wqkv_b", "L0_attn_out_w", "L0_attn_out_b",
        "L0_ffn_gate_weight", "L0_ffn_wi", "L0_ffn_wo"]


def kernel(**inputs):
    import numpy as _np
    import concourse.bacc as _bacc
    from concourse import mybir as _mybir
    from concourse.bass_utils import run_bass_kernel_spmd as _run

    nc = _bacc.Bacc("TRN2", target_bir_lowering=False, num_devices=1)
    arrays, args = {}, []
    for name in _INS:
        a = _np.ascontiguousarray(inputs[name])
        arrays[f"in_{name}"] = a
        args.append(nc.dram_tensor(f"in_{name}", a.shape, _mybir.dt.from_np(a.dtype), kind="ExternalInput").ap())
    shape = arrays["in_" + _INS[0]].shape
    args.append(nc.dram_tensor("out_0", shape, _mybir.dt.float32, kind="ExternalOutput").ap())
    transformer_block(nc, *args)
    r = _run(nc, [arrays], core_ids=[0])
    return r.results[0]["out_0"]
```
